# Optimizing a Trainium2 kernel written in Bass

```python
import numpy as np
import jax
import jax.numpy as jnp

def _softmax(x, axis=-1):
    return jax.nn.softmax(x, axis=axis)

def _gelu(x):
    return jax.nn.gelu(x, approximate=True)

def _silu(x):
    return jax.nn.silu(x)

def _sigmoid(x):
    return jax.nn.sigmoid(x)

def _layernorm(x, axis=-1, eps=1e-05):
    m = jnp.mean(x, axis=axis, keepdims=True)
    v = jnp.var(x, axis=axis, keepdims=True)
    return (x - m) / jnp.sqrt(v + eps)

def _scatter_add(tgt, idx, src, axis=0):
    return tgt.at[idx].add(src)

def _segment_sum(src, seg, n):
    return jax.ops.segment_sum(src, seg, n)
kernel_name = 'mk_vit_tower_d1_tok_img768_r4_1b4a77'

def setup_inputs(seed: int=0):
    np.random.seed(seed)
    _w = jnp.asarray

    def _rec_inputs():
        import jax
        import jax.numpy as jnp
        _rk = jax.random.key(seed)
        x = -4.65018e-05 + 0.999886 * jax.random.normal(jax.random.fold_in(_rk, 1), (32, 3, 96, 96), jnp.float32)
        return x
    x = _rec_inputs()

    def _L0_tok_setup():
        import jax, jax.numpy as jnp
        import numpy as np
        PATCH = 16
        key = jax.random.key(seed)
        ks = jax.random.split(key, 5)
        bs, C, H, W = (64, 3, 128, 128)
        R, E, P2 = (5, 192, PATCH * PATCH)
        x = jax.random.normal(ks[0], (bs, C, H, W), dtype=jnp.float32)
        W_repr = jax.random.normal(ks[1], (R, C), dtype=jnp.float32) * (1.0 / np.sqrt(C))
        b_repr = jax.random.normal(ks[2], (R,), dtype=jnp.float32) * 0.02
        W_proj = jax.random.normal(ks[3], (R, E, P2), dtype=jnp.float32) * (1.0 / np.sqrt(P2))
        b_proj = jax.random.normal(ks[4], (R, E), dtype=jnp.float32) * 0.02
        return {'x': x, 'W_repr': W_repr, 'b_repr': b_repr, 'W_proj': W_proj, 'b_proj': b_proj}
    _L0_tok_all = _L0_tok_setup()
    _L0_tok_in = {k: v for k, v in _L0_tok_all.items() if k in ('W_repr', 'b_repr', 'W_proj', 'b_proj')}
    del _L0_tok_all

    def _L0_attn_setup():
        import jax, jax.numpy as jnp
        import numpy as np
        DIM = 192
        NUM_HEADS = 12
        DIM_HEAD = 64
        SCALE = 1.0 / DIM_HEAD ** 0.5
        key = jax.random.key(seed)
        k1, k2, k3 = jax.random.split(key, 3)
        x = jax.random.normal(k1, (8, 256, DIM), dtype=jnp.float32)
        W_qkv = jax.random.normal(k2, (3 * NUM_HEADS * DIM_HEAD, DIM), dtype=jnp.float32) * 0.02
        W_out = jax.random.normal(k3, (DIM, NUM_HEADS * DIM_HEAD), dtype=jnp.float32) * 0.02
        return {'x': x, 'W_qkv': W_qkv, 'W_out': W_out}
    _L0_attn_all = _L0_attn_setup()
    _L0_attn_in = {k: v for k, v in _L0_attn_all.items() if k in ('W_qkv', 'W_out')}
    del _L0_attn_all

    def _L0_ffn_setup():
        import jax, jax.numpy as jnp
        import numpy as np
        B, S, D, E = (8, 256, 192, 8)
        F = 4 * D
        key = jax.random.key(seed)
        ks = jax.random.split(key, 5)
        scale = 0.02
        x = jax.random.normal(ks[0], (B, S, D), jnp.float32)
        gate_w = jax.random.normal(ks[1], (D, E), jnp.float32) * scale
        gate_b = jnp.zeros((E,), jnp.float32)
        w1 = jax.random.normal(ks[2], (E, D, F), jnp.float32) * scale
        b1 = jnp.zeros((E, F), jnp.float32)
        w2 = jax.random.normal(ks[3], (E, F, D), jnp.float32) * scale
        b2 = jnp.zeros((E, D), jnp.float32)
        return {'x': x, 'gate_w': gate_w, 'gate_b': gate_b, 'w1': w1, 'b1': b1, 'w2': w2, 'b2': b2}
    _L0_ffn_all = _L0_ffn_setup()
    _L0_ffn_in = {k: v for k, v in _L0_ffn_all.items() if k in ('gate_w', 'gate_b', 'w1', 'b1', 'w2', 'b2')}
    del _L0_ffn_all
    return {'x': x, 'L0_tok_W_repr': _L0_tok_in['W_repr'], 'L0_tok_b_repr': _L0_tok_in['b_repr'], 'L0_tok_W_proj': _L0_tok_in['W_proj'], 'L0_tok_b_proj': _L0_tok_in['b_proj'], 'L0_attn_W_qkv': _L0_attn_in['W_qkv'], 'L0_attn_W_out': _L0_attn_in['W_out'], 'L0_ffn_gate_w': _L0_ffn_in['gate_w'], 'L0_ffn_gate_b': _L0_ffn_in['gate_b'], 'L0_ffn_w1': _L0_ffn_in['w1'], 'L0_ffn_b1': _L0_ffn_in['b1'], 'L0_ffn_w2': _L0_ffn_in['w2'], 'L0_ffn_b2': _L0_ffn_in['b2']}

def reference(x, L0_tok_W_repr, L0_tok_b_repr, L0_tok_W_proj, L0_tok_b_proj, L0_attn_W_qkv, L0_attn_W_out, L0_ffn_gate_w, L0_ffn_gate_b, L0_ffn_w1, L0_ffn_b1, L0_ffn_w2, L0_ffn_b2):
    import jax
    import jax.numpy as jnp

    def _L0_tok_ref(x, W_repr, b_repr, W_proj, b_proj):
        import jax, jax.numpy as jnp
        import numpy as np
        PATCH = 16
        bs, C, H, W = x.shape
        R = W_repr.shape[0]
        ph = pw = PATCH
        h, w = (H // ph, W // pw)
        y = jnp.einsum('bchw,rc->bhwr', x, W_repr) + b_repr
        y = y.reshape(bs, h, ph, w, pw, R)
        y = y.transpose(5, 0, 1, 3, 2, 4).reshape(R, bs, h * w, ph * pw)
        out = jnp.einsum('rbnp,rep->bne', y, W_proj) + b_proj.sum(axis=0)
        return out

    def _L0_attn_ref(x, W_qkv, W_out):
        import jax, jax.numpy as jnp
        import numpy as np
        DIM = 192
        NUM_HEADS = 12
        DIM_HEAD = 64
        SCALE = 1.0 / DIM_HEAD ** 0.5
        B, T, _ = x.shape
        qkv = x @ W_qkv.T
        qkv = qkv.reshape(B, T, 3, NUM_HEADS, DIM_HEAD)
        q, k, v = (qkv[:, :, i].transpose(0, 2, 1, 3) for i in range(3))
        logits = jnp.einsum('bhtd,bhsd->bhts', q, k) / SCALE
        att = jax.nn.softmax(logits, axis=-1)
        o = jnp.einsum('bhts,bhsd->bhtd', att, v)
        cat = o.transpose(0, 2, 1, 3).reshape(B, T, NUM_HEADS * DIM_HEAD)
        return cat @ W_out.T

    def _L0_ffn_ref(x, gate_w, gate_b, w1, b1, w2, b2):
        import jax, jax.numpy as jnp
        import numpy as np
        B, S, D, E = (8, 256, 192, 8)
        F = 4 * D
        orig_shape = x.shape
        xt = x.reshape(-1, x.shape[-1])
        gates = jax.nn.softmax(xt @ gate_w + gate_b, axis=-1)
        expert_idx = jnp.argmax(gates, axis=-1)
        out = jnp.zeros_like(xt)
        n_experts = w1.shape[0]
        for e in range(n_experts):
            h = jax.nn.gelu(xt @ w1[e] + b1[e], approximate=False)
            y = h @ w2[e] + b2[e]
            out = jnp.where((expert_idx == e)[:, None], y, out)
        return out.reshape(orig_shape)
    h = _L0_tok_ref(x, L0_tok_W_repr, L0_tok_b_repr, L0_tok_W_proj, L0_tok_b_proj)
    h = h + _L0_attn_ref(_layernorm(h, axis=-1), L0_attn_W_qkv, L0_attn_W_out)
    h = h + _L0_ffn_ref(_layernorm(h, axis=-1), L0_ffn_gate_w, L0_ffn_gate_b, L0_ffn_w1, L0_ffn_b1, L0_ffn_w2, L0_ffn_b2)
    return h

_drawn_inputs = setup_inputs


def setup_inputs(seed=0):
    import zlib

    import numpy as np

    out = dict(_drawn_inputs(seed))
    spreads = {'L0_ffn_gate_b': (0.0, 0.1), 'L0_ffn_b1': (0.0, 0.726), 'L0_ffn_b2': (0.0, 0.1)}
    factors = {'L0_tok_b_repr': 2.759, 'L0_tok_b_proj': 3.134}
    for name, (base, spread) in spreads.items():
        noise = np.random.default_rng([zlib.crc32(name.encode()), seed]).standard_normal(out[name].shape)
        drawn = base * np.exp(spread * noise) if base else spread * noise
        out[name] = jnp.asarray(drawn.astype(out[name].dtype))
    for name, factor in factors.items():
        out[name] = (out[name] * factor).astype(out[name].dtype)
    return out
```

```python
from contextlib import ExitStack

import numpy as np

import concourse.bass as bass
from concourse import mybir

ALU = mybir.AluOpType
ACT = mybir.ActivationFunctionType
AX = mybir.AxisListType
F32 = mybir.dt.float32
BF16 = mybir.dt.bfloat16
U32 = mybir.dt.uint32
I32 = mybir.dt.int32

IMAGES, CHANNELS, SIDE, PATCH = 32, 3, 96, 16
GRID = SIDE // PATCH
PER_IMAGE = GRID * GRID
TOKENS = IMAGES * PER_IMAGE
REPR, D = 5, 192
HEADS, DH = 12, 64
HD = HEADS * DH
EXPERTS, FF = 8, 768
P = 128

NB = 4
BT = TOKENS // NB
TT = 96
NT = BT // TT
KX = CHANNELS * PATCH * PATCH // P
DA, DB = 128, 64
PAIRS = HEADS // 2
GROUPS = [(0, 108), (108, 108), (216, 72)]
GMAX = 108
HQ = 4
UNITS = [(q, g) for q in range(HEADS // HQ) for g in range(len(GROUPS))]
NU = len(UNITS)
LAG_T, LAG_AV = 2, 3
EPS = 1e-5
LOGIT_SCALE = 8.0
MASKED = -1.0e30

SLOT = 128
FFT = (TOKENS + EXPERTS * (SLOT - 1)) // SLOT
FCH = FF // P
SPARE_ROW = TOKENS
LISTS = EXPERTS * TOKENS
SPARE_SLOTS = 3 * P
PERM_COLS = (LISTS + SPARE_SLOTS) // P

ACC = [0, 1, 2, 3]
SC_BANK, TR_BANK, AV_BANK = 4, 5, 6


def per_block_products(last):
    order = []
    for s in range(2 * len(GROUPS)):
        order += step_products(s)
    if not last:
        order += [("tok", t) for t in range(NT)]
        order += [("xt", t) for t in range(NT)] + [("q", 0), ("k", 0)]
    order += [("o", t) for t in range(NT)]
    if not last:
        order += [("q", 1), ("k", 1)]
        order += [("gt", 0), ("v", 0, 0), ("gt", 1), ("v", 0, 1), ("gt", 2), ("v", 1, 0), ("v", 1, 1),
                  ("lg",), ("v", 2, 0), ("v", 2, 1), ("rk",)]
    else:
        order += [("gt", 0), ("gt", 1), ("gt", 2), ("lg",), ("rk",)]
    return order


def step_products(s):
    c = 2 * (s // 3 + 1)
    return [[("q", c), ("k", c)], [("q", c + 1)], [("k", c + 1)]][s % 3]


OPENING = ([("bias",)] + [("tok", t) for t in range(NT)] + [("xt", t) for t in range(NT)]
           + [("q", 0), ("k", 0), ("q", 1), ("k", 1)] + [("v", g, f) for g in range(3) for f in range(2)])
MIDDLE, FINAL = per_block_products(False), per_block_products(True)
assert len(MIDDLE) % len(ACC) == 0


def product(key, b, opening=False):
    if opening:
        n, blocks = OPENING.index(key), 0
    elif isinstance(b, int) and b == NB - 1:
        n, blocks = len(OPENING) + FINAL.index(key), b
    else:
        n, blocks = len(OPENING) + MIDDLE.index(key), b
    return n % len(ACC), n // len(ACC) + blocks * (len(MIDDLE) // len(ACC))


def build(nc, xT, w_proj, w_repr, b_repr, b_proj, w_qkv, w_out, gate_w, gate_b, w1, b1, w2, b2, out):
    table = nc.dram_tensor("token_table", [TOKENS + 1, 2 * D], F32, kind="Internal").ap()
    perm = nc.dram_tensor("expert_lists", [LISTS + SPARE_SLOTS, 1], U32, kind="Internal").ap()

    with ExitStack() as ctx:
        def sb(name, shape, dt=F32):
            return ctx.enter_context(nc.sbuf_tensor(name, shape, dt))

        def sem(name):
            return ctx.enter_context(nc.semaphore(name))

        psum = ctx.enter_context(nc.psum_tensor("psum", [P, 8, 512], F32))

        wp = sb("wp", [P, 2, REPR, D])
        wr = sb("wr", [P, REPR * CHANNELS])
        br = sb("br", [P, REPR])
        bp = sb("bp", [REPR, D])
        weff = sb("weff", [P, CHANNELS, 2, D])
        wb = sb("wb", [P, 2, D])
        bias = sb("bias", [TT, D])
        wqA = sb("wqA", [DA, 3 * HD])
        wqB = sb("wqB", [DB, 3 * HD])
        wo = sb("wo", [P, PAIRS, D])
        gwA = sb("gwA", [DA, EXPERTS])
        gwB = sb("gwB", [DB + 1, EXPERTS])
        w1A = sb("w1A", [DA, EXPERTS, FF])
        w1B = sb("w1B", [DB + 1, EXPERTS, FF])
        w2s = sb("w2s", [P, EXPERTS, FCH, D])
        b2s = sb("b2s", [P, EXPERTS, D])
        ident = sb("ident", [P, P])
        ones = sb("ones", [P, TT])
        mask = sb("mask", [GMAX, GMAX])
        before = sb("before", [TT, TT], BF16)
        all1 = sb("all1", [TT, TT], BF16)
        minus_half = sb("minus_half", [TT, 1])
        iota_i = sb("iota_i", [TT, 16], I32)
        iota = sb("iota", [TT, 16])
        tok_i = sb("tok_i", [TT, NT], I32)
        tok_f = sb("tok_f", [TT, NT])
        xb = sb("xb", [P, KX, BT])
        h = sb("h", [TT, NT, D])
        hres = sb("hres", [TT, NT, D])
        xn = sb("xn", [TT, NT, D])
        xnA = sb("xnA", [DA, BT])
        xnB = sb("xnB", [DB, BT])
        qT = sb("qT", [P, PAIRS, BT])
        kT = sb("kT", [P, PAIRS, 2 * BT])
        v = sb("v", [GMAX, len(GROUPS), HD])
        probs = sb("probs", [GMAX, 3, HQ * GMAX])
        probsT = sb("probsT", [GMAX, 3, HQ * GMAX])
        oT = sb("oT", [P, PAIRS, BT])
        top = sb("top", [GMAX, 3, HQ])
        total = sb("total", [GMAX, 3, HQ])
        share = sb("share", [GMAX, 3, HQ])
        rows = sb("rows", [TT, NT, 2 * D])
        xn2A = sb("xn2A", [DA, BT])
        xn2B = sb("xn2B", [DB + 1, BT])
        stats = sb("stats", [TT, 2, NT, 6])
        mv = sb("mv", [TT, 2, NT, 2])
        veps = sb("veps", [TT, 2, NT])
        rstd = sb("rstd", [TT, 2, NT])
        lg = sb("lg", [TT, NT, EXPERTS])
        lgmax = sb("lgmax", [TT, NT, 8])
        lgidx = sb("lgidx", [TT, NT, 8], U32)
        chosen = sb("chosen", [TT, NT])
        onehot = sb("onehot", [TT, NT, EXPERTS], BF16)
        place = sb("place", [TT, NT, EXPERTS])
        place_f = sb("place_f", [TT, NT])
        place_i = sb("place_i", [TT, NT], U32)
        tok_id = sb("tok_id", [TT, NT], U32)
        filled = sb("filled", [TT, EXPERTS])
        steps9 = sb("steps9", [1, EXPERTS, 9])
        cnt = sb("cnt", [1, EXPERTS])
        ntile = sb("ntile", [1, EXPERTS])
        tend = sb("tend", [1, EXPERTS])
        off = sb("off", [1, EXPERTS])
        grid = sb("grid", [1, FFT, EXPERTS])
        grid2 = sb("grid2", [1, FFT, EXPERTS])
        te = sb("te", [1, FFT])
        te7 = sb("te7", [1, FFT])
        tr = sb("tr", [1, FFT])
        tr2 = sb("tr2", [1, FFT])
        tile_expert = sb("tile_expert", [1, FFT], I32)
        tile_row = sb("tile_row", [1, FFT], I32)
        ids = sb("ids", [SLOT, FFT], U32)
        zeros = sb("zeros", [1, 2 * D])
        spare = sb("spare", [P, PERM_COLS], U32)
        xg = [t[:, :] for t in (sb("xg0", [SLOT, 2 * D]), sb("xg1", [SLOT, 2 * D]))]
        xbf = xb[:, :, :].rearrange("p k n -> p (k n)")
        xg += [xbf[:, 0:2 * D], xbf[:, 2 * D:4 * D]]
        fxA = [xn2A[:, 0:SLOT], xn2A[:, SLOT:2 * SLOT]]
        fxB = [xn2B[:, 0:SLOT], xn2B[:, SLOT:2 * SLOT]]
        qTf = qT[:, :, :].rearrange("p k n -> p (k n)")
        kTf = kT[:, :, :].rearrange("p k n -> p (k n)")
        oTf = oT[:, :, :].rearrange("p k n -> p (k n)")
        hid = [qTf[:, 0:FF], qTf[:, FF:2 * FF]]
        hidT = [kTf[:, 0:FF], kTf[:, FF:2 * FF]]
        res = [oTf[:, i * D:(i + 1) * D] for i in range(4)]
        yo = [oTf[:, (4 + i) * D:(5 + i) * D] for i in range(4)]

        x_here = sem("x_here")
        wp_here = sem("wp_here")
        wq_here = sem("wq_here")
        wo_here = sem("wo_here")
        w12_here = sem("w12_here")
        inits_out = sem("inits_out")
        full = [sem(f"acc_full{i}") for i in ACC]
        free = [sem(f"acc_free{i}") for i in ACC]
        sc_full, sc_free = sem("sc_full"), sem("sc_free")
        tr_full, tr_free = sem("tr_full"), sem("tr_free")
        av_full, av_free = sem("av_full"), sem("av_free")
        top_ready = sem("top_ready")
        shifted = sem("shifted")
        exp_ready = sem("exp_ready")
        share_ready = sem("share_ready")
        probs_ready = sem("probs_ready")
        ln_stats = sem("ln_stats")
        ln_rstd = sem("ln_rstd")
        xn_ready = sem("xn_ready")
        rows_ready = sem("rows_ready")
        hres_ready = sem("hres_ready")
        onehot_ready = sem("onehot_ready")
        place_ready = sem("place_ready")
        rows_sent = sem("rows_sent")
        lists_sent = sem("lists_sent")
        dve_step = sem("dve_step")
        pool_step = sem("pool_step")
        waited = {"dve": sem("dve_waited"), "pool": sem("pool_waited")}
        consts_ready = sem("consts_ready")
        weff_ready = sem("weff_ready")
        tiles_ready = sem("tiles_ready")
        ids_here = [sem(f"ids_here{j}") for j in range(FFT)]
        xg_here = [sem(f"xg_here{i}") for i in range(4)]
        fxt_full, fx_ready = sem("fxt_full"), sem("fx_ready")
        up_full, hid_ready = sem("up_full"), sem("hid_ready")
        hidt_full, hidt_ready = sem("hidt_full"), sem("hidt_ready")
        down_full, y_ready = sem("down_full"), sem("y_ready")
        res_ready = sem("res_ready")
        yo_free = sem("yo_free")
        out_sent = [sem(f"out_sent{i}") for i in range(4)]

        def acc(bank):
            return psum[:, ACC[bank], :]

        def taken(eng, slot):
            bank, before_it = slot
            eng.wait_ge(free[bank], before_it + 1)

        def all_taken(eng, keys, b, opening=False, following=None):
            last = {}
            for key in keys:
                last[product(key, b, opening)[0]] = product(key, b, opening)
            for bank, slot in last.items():
                if following is None or bank != following[0]:
                    taken(eng, slot)

        def complete(eng, slot):
            bank, before_it = slot
            eng.wait_ge(full[bank], before_it + 1)

        def passed(name, eng):
            eng.sem_inc(waited[name], 1)

        def unit(u):
            q, g = UNITS[u]
            return (q, g) + GROUPS[g]

        block = ctx.enter_context(nc.Block())

        @block.sync
        def _(sp):
            sp.sem_inc(rows_sent, 16)
            sp.dma_start(wp[:, :, :, :], w_proj).then_inc(wp_here, 16)
            sp.dma_start(wr[:, :], w_repr.partition_broadcast(P)).then_inc(wp_here, 16)
            sp.dma_start(br[:, :], b_repr.partition_broadcast(P)).then_inc(wp_here, 16)
            sp.dma_start(bp[:, :], b_proj).then_inc(wp_here, 16)
            sp.dma_start(xb[:, :, :], xT[0]).then_inc(x_here, 16)
            sp.dma_start(wqA[:, :], w_qkv[0:DA, :]).then_inc(wq_here, 16)
            sp.dma_start(wqB[:, :], w_qkv[DA:D, :]).then_inc(wq_here, 16)
            sp.dma_start(wo[:, :, :], w_out).then_inc(wo_here, 16)
            sp.dma_start(gwA[:, :], gate_w[0:DA, :]).then_inc(wo_here, 16)
            sp.dma_start(gwB[0:DB, :], gate_w[DA:D, :]).then_inc(wo_here, 16)
            sp.dma_start(gwB[DB:DB + 1, :], gate_b).then_inc(wo_here, 16)
            sp.wait_ge(consts_ready, 1)
            sp.dma_start(perm.rearrange("(p c) o -> p (c o)", c=PERM_COLS), spare[:, :]).then_inc(inits_out, 16)
            sp.dma_start(table[SPARE_ROW:SPARE_ROW + 1, :], zeros[:, :]).then_inc(inits_out, 16)

            def body(b, last):
                if not last:
                    sp.wait_ge(xn_ready, NT * b + NT)
                    sp.dma_start(xb[:, :, :], xT[b + 1]).then_inc(x_here, 16)
                sp.wait_ge(rows_ready, NT * b + NT + 1)
                sp.dma_start(table[bass.ds(b * BT, BT), :].rearrange("(t p) d -> p t d", p=TT),
                             rows[:, :, :]).then_inc(rows_sent, 16)

            with sp.Fori(0, NB - 1) as b:
                body(b, False)
            body(NB - 1, True)

            sp.wait_ge(rows_sent, 16 * NB + 16)
            sp.wait_ge(lists_sent, 16 * NT * (NB + 1))
            sp.wait_ge(tiles_ready, 1)
            for j in range(FFT):
                row = sp.value_load(tile_row[0:1, j:j + 1], min_val=0, max_val=LISTS)
                sp.dma_start(ids[:, j:j + 1], perm[bass.ds(row, SLOT), :]).then_inc(ids_here[j], 16)

        @block.tensor
        def _(pe):
            def into(slot):
                bank, before_it = slot
                pe.wait_ge(free[bank], before_it)
                return acc(bank)

            def tokens(t, slot):
                dst = into(slot)
                for k in range(KX):
                    mm = pe.matmul(dst[0:TT, 0:D], xb[:, k, t * TT:(t + 1) * TT], weff[:, k // 2, k % 2, :],
                                   start=(k == 0), stop=(k == KX - 1))
                mm.then_inc(full[slot[0]], 1)

            def turn_xn(t, slot, ready, src, col):
                dst = into(slot)
                pe.wait_ge(*ready)
                pe.transpose(dst[0:DA, 0:TT], src[:, t, col:col + DA], ident[0:TT, 0:TT])
                pe.transpose(dst[0:DB, TT:2 * TT], src[:, t, col + DA:col + D],
                             ident[0:TT, 0:TT]).then_inc(full[slot[0]], 1)

            def heads(which, c, slot):
                dst = into(slot)
                col = (0 if which == "q" else HD) + c * P
                pe.matmul(dst[:, 0:BT], wqA[:, col:col + P], xnA[:, :], start=True, stop=False)
                pe.matmul(dst[:, 0:BT], wqB[:, col:col + P], xnB[:, :], start=False,
                          stop=True).then_inc(full[slot[0]], 1)

            def values(g, f, slot):
                dst = into(slot)
                t0, n = GROUPS[g]
                col = 2 * HD + f * (HD // 2)
                pe.matmul(dst[0:n, 0:HD // 2], xnA[:, t0:t0 + n], wqA[:, col:col + HD // 2], start=True, stop=False)
                pe.matmul(dst[0:n, 0:HD // 2], xnB[:, t0:t0 + n], wqB[:, col:col + HD // 2], start=False,
                          stop=True).then_inc(full[slot[0]], 1)

            def scores(u, b):
                q, g, t0, n = unit(u)
                pe.wait_ge(sc_free, NU * b + u + 1)
                for i in range(2):
                    c = 2 * q + i
                    mm = pe.matmul(psum[0:n, SC_BANK, 2 * i * n:2 * (i + 1) * n], qT[:, c, t0:t0 + n],
                                   kT[:, c, 2 * t0:2 * (t0 + n)], start=True, stop=True)
                mm.then_inc(sc_full, 1)

            def turn_probs(u, b):
                q, g, t0, n = unit(u)
                pe.wait_ge(probs_ready, NU * b + u + 1)
                pe.wait_ge(tr_free, NU * b + u + 1)
                for i in range(HQ):
                    mm = pe.transpose(psum[0:n, TR_BANK, i * n:(i + 1) * n], probs[0:n, u % 3, i * n:(i + 1) * n],
                                      ident[0:n, 0:n])
                mm.then_inc(tr_full, 1)

            def attend(u, b):
                q, g, t0, n = unit(u)
                pe.wait_ge(tr_free, NU * b + u + 2)
                pe.wait_ge(av_free, NU * b + u + 1)
                for i in range(2):
                    c = 2 * q + i
                    mm = pe.matmul(psum[:, AV_BANK, 2 * i * n:2 * (i + 1) * n], v[0:n, g, c * P:(c + 1) * P],
                                   probsT[0:n, u % 3, 2 * i * n:2 * (i + 1) * n], start=True, stop=True)
                mm.then_inc(av_full, 1)

            def project(t, slot, b):
                dst = into(slot)
                pe.wait_ge(av_free, NU * b + NU + 1)
                for c in range(PAIRS):
                    mm = pe.matmul(dst[0:TT, 0:D], oT[:, c, t * TT:(t + 1) * TT], wo[:, c, :],
                                   start=(c == 0), stop=(c == PAIRS - 1))
                mm.then_inc(full[slot[0]], 1)

            def gate(b):
                slot = product(("lg",), b)
                all_taken(pe, [("gt", t) for t in range(NT)], b, following=slot)
                dst = into(slot)
                for t in range(NT):
                    pe.matmul(dst[0:TT, t * EXPERTS:(t + 1) * EXPERTS], xn2A[:, t * TT:(t + 1) * TT], gwA[:, :],
                              start=True, stop=False)
                    mm = pe.matmul(dst[0:TT, t * EXPERTS:(t + 1) * EXPERTS], xn2B[:, t * TT:(t + 1) * TT], gwB[:, :],
                                   start=False, stop=True)
                mm.then_inc(full[slot[0]], 1)

            def ranks(b):
                slot = product(("rk",), b)
                dst = into(slot)
                pe.wait_ge(onehot_ready, b + 1)
                for t in range(NT):
                    col = t * EXPERTS
                    for e in range(t):
                        pe.matmul(dst[0:TT, col:col + EXPERTS], all1[:, :], onehot[:, e, :],
                                  start=(e == 0), stop=False)
                    pe.matmul(dst[0:TT, col:col + EXPERTS], before[:, :], onehot[:, t, :], start=(t == 0), stop=True)
                col = NT * EXPERTS
                for t in range(NT):
                    mm = pe.matmul(dst[0:TT, col:col + EXPERTS], all1[:, :], onehot[:, t, :],
                                   start=(t == 0), stop=(t == NT - 1))
                mm.then_inc(full[slot[0]], 1)

            pe.wait_ge(consts_ready, 1)
            pe.wait_ge(weff_ready, 1)
            slot = product(("bias",), 0, opening=True)
            dst = into(slot)
            pe.matmul(dst[0:TT, 0:D], ones[:, :], wb[:, 0, :], start=True, stop=False)
            pe.matmul(dst[0:TT, 0:D], ones[:, :], wb[:, 1, :], start=False, stop=False)
            pe.matmul(dst[0:TT, 0:D], ones[0:REPR, :], bp[:, :], start=False, stop=True).then_inc(full[slot[0]], 1)
            pe.wait_ge(x_here, 16)
            pe.wait_ge(weff_ready, 2)
            for t in range(NT):
                tokens(t, product(("tok", t), 0, opening=True))
            for t in range(NT):
                turn_xn(t, product(("xt", t), 0, opening=True), (xn_ready, t + 1), xn, 0)
            pe.wait_ge(wq_here, 32)
            all_taken(pe, [("xt", t) for t in range(NT)], 0, opening=True)
            for c in range(2):
                heads("q", c, product(("q", c), 0, opening=True))
                heads("k", c, product(("k", c), 0, opening=True))
            for g in range(3):
                for f in range(2):
                    values(g, f, product(("v", g, f), 0, opening=True))

            def start_taken(b, opening):
                all_taken(pe, [(w, c) for c in range(2) for w in "qk"] +
                          [("v", g, f) for g in range(3) for f in range(2)], b, opening)

            def body(b, last):
                for s in range(NU + LAG_AV):
                    if s < NU:
                        if s in (3, 6):
                            all_taken(pe, [(w, c) for c in (2 * (s // 3), 2 * (s // 3) + 1) for w in "qk"], b)
                        scores(s, b)
                    if s < 6:
                        for w, c in step_products(s):
                            heads(w, c, product((w, c), b))
                    elif s < 9 and not last:
                        if s == 6:
                            pe.wait_ge(x_here, 16 * b + 32)
                        tokens(s - 6, product(("tok", s - 6), b))
                    if LAG_T <= s < NU + LAG_T:
                        turn_probs(s - LAG_T, b)
                    if s >= LAG_AV:
                        attend(s - LAG_AV, b)
                    if s >= 9 and not last:
                        for t in [[0, 1], [2], []][s - 9]:
                            turn_xn(t, product(("xt", t), b), (xn_ready, NT * b + NT + t + 1), xn, 0)
                        if s == 10:
                            slot = product(("q", 0), b)
                            all_taken(pe, [("xt", t) for t in range(NT)], b, following=slot)
                            heads("q", 0, slot)
                        if s == 11:
                            heads("k", 0, product(("k", 0), b))
                pe.wait_ge(wo_here, 64)
                for t in range(NT):
                    project(t, product(("o", t), b), b)
                if not last:
                    heads("q", 1, product(("q", 1), b))
                    heads("k", 1, product(("k", 1), b))
                for t in range(NT):
                    turn_xn(t, product(("gt", t), b), (rows_ready, NT * b + t + 2), rows, D)
                    if not last:
                        for g, f in [[(0, 0)], [(0, 1)], [(1, 0), (1, 1)]][t]:
                            values(g, f, product(("v", g, f), b))
                gate(b)
                if not last:
                    values(2, 0, product(("v", 2, 0), b))
                    values(2, 1, product(("v", 2, 1), b))
                ranks(b)
                if not last:
                    start_taken(b, False)

            start_taken(0, True)
            with pe.Fori(0, NB - 1) as b:
                body(b, False)
            body(NB - 1, True)

            def turn_x(r, i):
                j = r * 4 + i
                pe.wait_ge(xg_here[i % 4], r * 16 + 16 * (i // 4 + 1))
                pe.wait_ge(fx_ready, j)
                pe.transpose(psum[0:DA, 7, 0:SLOT], xg[i % 4][:, D:D + DA], ident[:, :])
                pe.transpose(psum[0:DB, 7, SLOT:2 * SLOT], xg[i % 4][:, D + DA:2 * D],
                             ident[:, :]).then_inc(fxt_full, 1)

            def up(r, i):
                j = r * 4 + i
                e = pe.value_load(tile_expert[0:1, bass.ds(j, 1)], min_val=0, max_val=EXPERTS - 1)
                pe.wait_ge(fx_ready, j + 1)
                p2 = i % 2
                for lo, hi in ((0, 512), (512, FF)):
                    dst = psum[:, 2 * p2 + lo // 512, 0:hi - lo]
                    pe.matmul(dst, fxA[p2], w1A[:, bass.ds(e, 1), lo:hi], start=True, stop=False)
                    mm = pe.matmul(dst, fxB[p2], w1B[:, bass.ds(e, 1), lo:hi], start=False, stop=True)
                mm.then_inc(up_full, 1)

            def turn_hidden(r, i):
                j = r * 4 + i
                pe.wait_ge(hid_ready, j + 1)
                pe.wait_ge(hidt_ready, j + 1)
                for c in range(FCH):
                    mm = pe.transpose(psum[:, 4 + c // 4, (c % 4) * P:(c % 4 + 1) * P],
                                      hid[i % 2][:, c * P:(c + 1) * P], ident[:, :])
                mm.then_inc(hidt_full, 1)

            def down(r, i):
                j = r * 4 + i
                e = pe.value_load(tile_expert[0:1, bass.ds(j, 1)], min_val=0, max_val=EXPERTS - 1)
                pe.wait_ge(hidt_ready, j + 2)
                pe.wait_ge(y_ready, j + 1)
                for c in range(FCH):
                    mm = pe.matmul(psum[:, 6, 0:D], hidT[i % 2][:, c * P:(c + 1) * P],
                                   w2s[:, bass.ds(e, 1), c, :], start=(c == 0), stop=(c == FCH - 1))
                mm.then_inc(down_full, 1)

            pe.wait_ge(tiles_ready, 1)
            pe.wait_ge(w12_here, 16 * 5)
            turn_x(0, 0)
            up(0, 0)
            turn_x(0, 1)

            def four_tiles(r, last):
                for i in range(4):
                    turn_hidden(r, i)
                    if not last or i < 3:
                        up(r, i + 1)
                    if not last or i < 2:
                        turn_x(r, i + 2)
                    down(r, i)

            with pe.Fori(0, FFT // 4 - 1) as r:
                four_tiles(r, False)
            four_tiles(FFT // 4 - 1, True)

        @block.scalar
        def _(act):
            act.sem_inc(tr_free, 1)
            act.sem_inc(av_free, 1)
            act.wait_ge(x_here, 16)
            act.dma_start(w1A[:, :, :], w1[0:DA, :, :]).then_inc(w12_here, 16)
            act.dma_start(w1B[0:DB, :, :], w1[DA:D, :, :]).then_inc(w12_here, 16)
            act.dma_start(w1B[DB:DB + 1, :, :], b1).then_inc(w12_here, 16)
            act.dma_start(w2s[:, :, :, :], w2).then_inc(w12_here, 16)
            act.dma_start(b2s[:, :, :], b2.partition_broadcast(P)).then_inc(w12_here, 16)

            def take_q(c, slot):
                complete(act, slot)
                act.copy(qT[:, c, :], acc(slot[0])[:, 0:BT]).then_inc(free[slot[0]], 1)

            def take_k(c, slot):
                complete(act, slot)
                src = acc(slot[0])
                for i in range(2):
                    rows_ = slice(DH * i, DH * (i + 1))
                    for t0, n, m in ((0, GMAX, 2), (2 * GMAX, BT - 2 * GMAX, 1)):
                        dst = kT[rows_, c, 2 * t0:2 * t0 + 2 * m * n].rearrange("p (g i n) -> p g i n", i=2, n=n)
                        cp = act.copy(dst[:, :, i, :], src[rows_, t0:t0 + m * n].rearrange("p (g n) -> p g n", n=n))
                cp.then_inc(free[slot[0]], 1)

            def take(w, c, slot):
                (take_q if w == "q" else take_k)(c, slot)

            act.wait_ge(consts_ready, 1)
            for c in range(2):
                for w in "qk":
                    take(w, c, product((w, c), 0, opening=True))

            def body(b, last):
                for s in range(NU + LAG_AV):
                    if s < 6:
                        for w, c in step_products(s):
                            take(w, c, product((w, c), b))
                    if LAG_T <= s < NU + LAG_T:
                        u = s - LAG_T
                        q, g, t0, n = unit(u)
                        act.wait_ge(tr_full, NU * b + u + 1)
                        act.copy(probsT[0:n, u % 3, 0:HQ * n], psum[0:n, TR_BANK, 0:HQ * n]).then_inc(tr_free, 1)
                    if s >= LAG_AV:
                        u = s - LAG_AV
                        q, g, t0, n = unit(u)
                        act.wait_ge(av_full, NU * b + u + 1)
                        src = psum[:, AV_BANK, 0:HQ * n].rearrange("p (c i n) -> p c i n", c=2, i=2)
                        for i in range(2):
                            rows_ = slice(DH * i, DH * (i + 1))
                            cp = act.copy(oT[rows_, 2 * q:2 * q + 2, t0:t0 + n], src[rows_, :, i, :])
                        cp.then_inc(av_free, 1)
                    if s < NU:
                        q, g, t0, n = unit(s)
                        act.wait_ge(shifted, NU * b + s + 1)
                        act.activation(probs[0:n, s % 3, 0:HQ * n], probs[0:n, s % 3, 0:HQ * n], ACT.Exp,
                                       scale=LOGIT_SCALE).then_inc(exp_ready, 1)
                    if s >= 10 and not last:
                        take("qk"[s - 10], 0, product(("qk"[s - 10], 0), b))
                if not last:
                    take("q", 1, product(("q", 1), b))
                    take("k", 1, product(("k", 1), b))
                for t in range(NT):
                    slot = product(("gt", t), b)
                    complete(act, slot)
                    act.copy(xn2A[:, t * TT:(t + 1) * TT], acc(slot[0])[:, 0:TT])
                    act.copy(xn2B[0:DB, t * TT:(t + 1) * TT],
                             acc(slot[0])[0:DB, TT:2 * TT]).then_inc(free[slot[0]], 1)

            with act.Fori(0, NB - 1) as b:
                body(b, False)
            body(NB - 1, True)

            def gelu(r, i):
                j = r * 4 + i
                act.wait_ge(up_full, j + 1)
                p2 = i % 2
                act.activation(hid[p2][:, 0:512], psum[:, 2 * p2, :], ACT.Gelu)
                act.activation(hid[p2][:, 512:FF], psum[:, 2 * p2 + 1, 0:FF - 512], ACT.Gelu).then_inc(hid_ready, 1)

            with act.Fori(0, FFT // 4) as r:
                for i in range(4):
                    gelu(r, i)

        @block.vector
        def _(dve):
            steps = [0, 0]

            def own(ins):
                ins.then_inc(dve_step, 1)
                steps[0] += 1
                dve.wait_ge(dve_step, steps[1] + steps[0])

            def layernorm_stats(src, kind, t, n_before):
                own(dve.bn_stats(stats[:, kind, t, :], src))
                passed("dve", dve)
                dve.bn_aggr(mv[:, kind, t, :], stats[:, kind, t, :]).then_inc(ln_stats, 1)

            def layernorm(dst, src, kind, t, n_before):
                dve.wait_ge(ln_rstd, n_before + 1)
                return dve.tensor_scalar(dst, src, mv[:, kind, t, 0:1], rstd[:, kind, t:t + 1],
                                         ALU.subtract, ALU.mult)

            def take_tokens(t, slot, n_before):
                complete(dve, slot)
                dve.tensor_tensor(h[:, t, :], acc(slot[0])[0:TT, 0:D], bias[:, :], ALU.add).then_inc(free[slot[0]], 1)
                taken(dve, slot)
                layernorm_stats(h[:, t, :], 0, t, n_before)

            def take_xnT(t, slot):
                complete(dve, slot)
                dve.tensor_copy(xnA[:, t * TT:(t + 1) * TT], acc(slot[0])[:, 0:TT])
                dve.tensor_copy(xnB[:, t * TT:(t + 1) * TT], acc(slot[0])[0:DB, TT:2 * TT]).then_inc(free[slot[0]], 1)

            def take_v(g, f, slot):
                t0, n = GROUPS[g]
                complete(dve, slot)
                dve.tensor_copy(v[0:n, g, f * (HD // 2):(f + 1) * (HD // 2)],
                                acc(slot[0])[0:n, 0:HD // 2]).then_inc(free[slot[0]], 1)

            dve.sem_inc(sc_free, 1)
            dve.sem_inc(rows_ready, 1)
            dve.sem_inc(hidt_ready, 1)
            dve.sem_inc(y_ready, 1)
            dve.memset(xn2B[DB:DB + 1, :], 1.0)
            dve.wait_ge(wp_here, 64)
            for r in range(REPR):
                if r == 0:
                    ins = dve.tensor_scalar(wb[:, :, :], wp[:, :, r, :], br[:, r:r + 1], None, ALU.mult)
                else:
                    ins = dve.scalar_tensor_tensor(wb[:, :, :], wp[:, :, r, :], br[:, r:r + 1], wb[:, :, :],
                                                   ALU.mult, ALU.add)
                own(ins)
            dve.engine_nop().then_inc(weff_ready, 1)
            for r in range(REPR):
                for c in range(CHANNELS):
                    s = r * CHANNELS + c
                    if r == 0:
                        ins = dve.tensor_scalar(weff[:, c, :, :], wp[:, :, r, :], wr[:, s:s + 1], None, ALU.mult)
                    else:
                        ins = dve.scalar_tensor_tensor(weff[:, c, :, :], wp[:, :, r, :], wr[:, s:s + 1],
                                                       weff[:, c, :, :], ALU.mult, ALU.add)
                own(ins)
            dve.engine_nop().then_inc(weff_ready, 1)
            slot = product(("bias",), 0, opening=True)
            complete(dve, slot)
            dve.tensor_copy(bias[:, :], acc(slot[0])[0:TT, 0:D]).then_inc(free[slot[0]], 1)
            taken(dve, slot)
            for t in range(NT):
                take_tokens(t, product(("tok", t), 0, opening=True), t)
            dve.wait_ge(consts_ready, 1)
            own(dve.tensor_copy(iota[:, :], iota_i[:, :]))
            dve.tensor_scalar(filled[:, :], iota[:, 0:EXPERTS], float(TOKENS), None, ALU.mult)
            own(dve.tensor_copy(tok_f[:, :], tok_i[:, :]))
            for t in range(NT):
                layernorm(xn[:, t, :], h[:, t, :], 0, t, t).then_inc(xn_ready, 1)
            for t in range(NT):
                take_xnT(t, product(("xt", t), 0, opening=True))
            for g in range(3):
                for f in range(2):
                    take_v(g, f, product(("v", g, f), 0, opening=True))
            before_blocks = steps[0]

            def body(b, last):
                steps[0] = 0
                steps[1] = before_blocks + b * OWN_PER_BLOCK
                lns = NT + b * 2 * NT

                def finish_sum(u):
                    q, g, t0, n = unit(u)
                    dve.wait_ge(exp_ready, NU * b + u + 1)
                    own(dve.tensor_reduce(total[0:n, u % 3, :], probs[0:n, u % 3, 0:HQ * n]
                                          .rearrange("p (h n) -> p h n", n=n), AX.X, ALU.add))
                    dve.reciprocal(share[0:n, u % 3, :], total[0:n, u % 3, :]).then_inc(share_ready, 1)

                for s in range(NU + 1):
                    if s < NU:
                        q, g, t0, n = unit(s)
                        dve.wait_ge(sc_full, NU * b + s + 1)
                        sc = probs[0:n, s % 3, 0:HQ * n].rearrange("p (h n) -> p h n", n=n)
                        dve.tensor_tensor(sc, psum[0:n, SC_BANK, 0:HQ * n].rearrange("p (h n) -> p h n", n=n),
                                          mask[0:n, 0:n].unsqueeze(1).to_broadcast([n, HQ, n]),
                                          ALU.add).then_inc(sc_free, 1)
                        dve.wait_ge(sc_free, NU * b + s + 2)
                        dve.tensor_reduce(top[0:n, s % 3, :], sc, AX.X, ALU.max).then_inc(top_ready, 1)
                    if s >= 1:
                        finish_sum(s - 1)
                    if not last:
                        if 7 <= s:
                            t = s - 7
                            layernorm(xn[:, t, :], h[:, t, :], 0, t, lns + t).then_inc(xn_ready, 1)
                        if 6 <= s < 9:
                            if s == 6:
                                dve.wait_ge(hres_ready, b + 1)
                            take_tokens(s - 6, product(("tok", s - 6), b), lns + s - 6)
                        if s == 9:
                            for t in range(NT):
                                take_xnT(t, product(("xt", t), b))
                if last:
                    lns -= NT
                dve.wait_ge(rows_sent, 16 * b + 16)
                for t in range(NT + 1):
                    if t < NT:
                        slot = product(("o", t), b)
                        complete(dve, slot)
                        dve.tensor_tensor(rows[:, t, 0:D], acc(slot[0])[0:TT, 0:D], hres[:, t, :],
                                          ALU.add).then_inc(free[slot[0]], 1)
                        taken(dve, slot)
                        layernorm_stats(rows[:, t, 0:D], 1, t, lns + NT + t)
                    if t >= 1:
                        layernorm(rows[:, t - 1, D:2 * D], rows[:, t - 1, 0:D], 1, t - 1,
                                  lns + NT + t - 1).then_inc(rows_ready, 1)
                if not last:
                    for g, f in ((0, 0), (0, 1), (1, 0), (1, 1)):
                        take_v(g, f, product(("v", g, f), b))
                slot = product(("lg",), b)
                complete(dve, slot)
                dve.tensor_copy(lg[:, :, :].rearrange("p t e -> p (t e)"),
                                acc(slot[0])[0:TT, 0:NT * EXPERTS]).then_inc(free[slot[0]], 1)
                taken(dve, slot)
                passed("dve", dve)
                for t in range(NT):
                    ins = dve.max(lgmax[:, t, :], lg[:, t, :])
                own(ins)
                passed("dve", dve)
                for t in range(NT):
                    ins = dve.max_index(lgidx[:, t, :], lgmax[:, t, :], lg[:, t, :])
                own(ins)
                own(dve.tensor_copy(chosen[:, :], lgidx[:, :, 0]))
                dve.tensor_tensor(onehot[:, :, :], iota[:, 0:EXPERTS].unsqueeze(1).to_broadcast([TT, NT, EXPERTS]),
                                  chosen[:, :].unsqueeze(2).to_broadcast([TT, NT, EXPERTS]),
                                  ALU.is_equal).then_inc(onehot_ready, 1)
                if not last:
                    for f in range(2):
                        take_v(2, f, product(("v", 2, f), b))
                slot = product(("rk",), b)
                complete(dve, slot)
                rk = acc(slot[0])
                own(dve.tensor_tensor(place[:, :, :], rk[0:TT, 0:NT * EXPERTS].rearrange("p (t e) -> p t e", t=NT),
                                      filled[:, :].unsqueeze(1).to_broadcast([TT, NT, EXPERTS]), ALU.add))
                dve.tensor_tensor(filled[:, :], rk[0:TT, NT * EXPERTS:(NT + 1) * EXPERTS], filled[:, :],
                                  ALU.add).then_inc(free[slot[0]], 1)
                own(dve.tensor_tensor(place[:, :, :], place[:, :, :], onehot[:, :, :], ALU.mult))
                own(dve.tensor_reduce(place_f[:, :], place[:, :, :], AX.X, ALU.add))
                dve.wait_ge(lists_sent, 16 * NT * (b + 1))
                dve.tensor_copy(tok_id[:, :], tok_f[:, :])
                dve.tensor_copy(place_i[:, :], place_f[:, :]).then_inc(place_ready, 1)
                own(dve.tensor_scalar(tok_f[:, :], tok_f[:, :], float(BT), None, ALU.add))
                if not last:
                    assert steps[0] == OWN_PER_BLOCK, steps[0]

            with dve.Fori(0, NB - 1) as b:
                body(b, False)
            body(NB - 1, True)

            e8 = iota[0:1, 0:EXPERTS]
            j16 = iota[0:1, 0:FFT].unsqueeze(2).to_broadcast([1, FFT, EXPERTS])

            def over_tiles(row):
                return row.unsqueeze(1).to_broadcast([1, FFT, EXPERTS])

            own(dve.scalar_tensor_tensor(cnt[:, :], e8, -float(TOKENS), filled[0:1, :], ALU.mult, ALU.add))
            own(dve.tensor_scalar(tr[:, 0:9], iota[0:1, 0:9], float(SLOT), None, ALU.mult))
            own(dve.tensor_tensor(steps9[:, :, :], cnt[:, :].unsqueeze(2).to_broadcast([1, EXPERTS, 9]),
                                  tr[:, 0:9].unsqueeze(1).to_broadcast([1, EXPERTS, 9]), ALU.is_gt))
            own(dve.tensor_reduce(ntile[:, :], steps9[:, :, :], AX.X, ALU.add))
            own(dve.tensor_tensor_scan(tend[:, :], ones[0:1, 0:EXPERTS], ntile[:, :], 0.0, ALU.mult, ALU.add))
            own(dve.tensor_tensor(off[:, :], tend[:, :], ntile[:, :], ALU.subtract))
            own(dve.tensor_scalar(off[:, :], off[:, :], -float(SLOT), None, ALU.mult))
            own(dve.scalar_tensor_tensor(off[:, :], e8, float(TOKENS), off[:, :], ALU.mult, ALU.add))
            own(dve.tensor_tensor(grid[:, :, :], over_tiles(tend[:, :]), j16, ALU.is_le))
            own(dve.tensor_reduce(te[:, :], grid[:, :, :], AX.X, ALU.add))
            own(dve.tensor_tensor(grid[:, :, :], over_tiles(e8), te[:, :].unsqueeze(2).to_broadcast([1, FFT, EXPERTS]),
                                  ALU.is_equal))
            own(dve.scalar_tensor_tensor(grid2[:, :, :], j16, float(SLOT), over_tiles(off[:, :]), ALU.mult, ALU.add))
            own(dve.tensor_tensor(grid2[:, :, :], grid2[:, :, :], grid[:, :, :], ALU.mult))
            own(dve.tensor_reduce(tr[:, :], grid2[:, :, :], AX.X, ALU.add))
            own(dve.tensor_scalar(tr2[:, :], te[:, :], float(EXPERTS), float(LISTS), ALU.is_ge, ALU.mult))
            own(dve.tensor_tensor(tr[:, :], tr[:, :], tr2[:, :], ALU.add))
            own(dve.tensor_scalar(te7[:, :], te[:, :], float(EXPERTS - 1), None, ALU.min))
            dve.tensor_copy(tile_row[:, :], tr[:, :])
            dve.memset(fxB[0][DB:DB + 1, :], 1.0)
            dve.memset(fxB[1][DB:DB + 1, :], 1.0)
            dve.tensor_copy(tile_expert[:, :], te7[:, :]).then_inc(tiles_ready, 1)
            dve.wait_ge(tiles_ready, 1)

            def take_x(r, i):
                j = r * 4 + i
                e = dve.value_load(tile_expert[0:1, bass.ds(j, 1)], min_val=0, max_val=EXPERTS - 1)
                dve.wait_ge(fxt_full, j + 1)
                dve.tensor_copy(fxA[i % 2], psum[0:DA, 7, 0:SLOT])
                dve.tensor_copy(fxB[i % 2][0:DB, :], psum[0:DB, 7, SLOT:2 * SLOT]).then_inc(fx_ready, 1)
                dve.tensor_tensor(res[i % 4], xg[i % 4][:, 0:D], b2s[:, bass.ds(e, 1), :].rearrange("p o d -> p (o d)"),
                                  ALU.add).then_inc(res_ready, 1)

            def take_hidden(r, i):
                j = r * 4 + i
                dve.wait_ge(hidt_full, j + 1)
                dve.tensor_copy(hidT[i % 2][:, 0:512], psum[:, 4, :])
                dve.tensor_copy(hidT[i % 2][:, 512:FF], psum[:, 5, 0:FF - 512]).then_inc(hidt_ready, 1)

            def finish(r, i):
                j = r * 4 + i
                dve.wait_ge(down_full, j + 1)
                dve.wait_ge(res_ready, j + 1)
                dve.wait_ge(yo_free, j + 1)
                dve.tensor_tensor(yo[i % 4], psum[:, 6, 0:D], res[i % 4], ALU.add).then_inc(y_ready, 1)

            dve.wait_ge(w12_here, 16 * 5)
            take_x(0, 0)
            take_x(0, 1)

            def four_tiles(r, last):
                for i in range(4):
                    take_hidden(r, i)
                    if not last or i < 2:
                        take_x(r, i + 2)
                    finish(r, i)

            with dve.Fori(0, FFT // 4 - 1) as r:
                four_tiles(r, False)
            four_tiles(FFT // 4 - 1, True)

        @block.gpsimd
        def _(pool):
            pools = [0]

            def own(ins):
                ins.then_inc(pool_step, 1)
                pools[0] += 1
                pool.wait_ge(pool_step, pools[0])

            pool.sem_inc(yo_free, 4)
            pool.memset(ones[:, :], 1.0)
            pool.memset(ident[:, :], 0.0)
            pool.memset(mask[:, :], 0.0)
            pool.memset(before[:, :], 1.0)
            pool.memset(all1[:, :], 1.0)
            pool.memset(minus_half[:, :], -0.5)
            pool.memset(zeros[:, :], 0.0)
            pool.memset(spare[:, :], SPARE_ROW)
            pool.iota(iota_i[:, :], pattern=[[1, 16]], base=0, channel_multiplier=0)
            pool.iota(place_i[:, :], pattern=[[TT, NT]], base=LISTS, channel_multiplier=1)
            pool.memset(tok_id[:, :], SPARE_ROW).then_inc(place_ready, 1)
            pool.iota(tok_i[:, :], pattern=[[TT, NT]], base=0, channel_multiplier=1)
            own(pool.memset(kT[:, :, :], 0.0))
            pool.affine_select(out=ident[:, :], in_=ident[:, :], compare_op=ALU.not_equal, fill=1.0, base=0,
                               pattern=[[-1, P]], channel_multiplier=1)
            pool.affine_select(out=before[:, :], in_=before[:, :], compare_op=ALU.is_gt, fill=0.0, base=0,
                               pattern=[[1, TT]], channel_multiplier=-1)
            images = GMAX // PER_IMAGE
            m3 = mask[:, :].rearrange("p (j n) -> p j n", n=PER_IMAGE)
            own(pool.affine_select(out=m3, in_=m3, compare_op=ALU.is_ge, fill=MASKED, base=0,
                                   pattern=[[-PER_IMAGE, images], [0, PER_IMAGE]], channel_multiplier=1))
            pool.affine_select(out=m3, in_=m3, compare_op=ALU.is_ge, fill=MASKED, base=PER_IMAGE - 1,
                               pattern=[[PER_IMAGE, images], [0, PER_IMAGE]],
                               channel_multiplier=-1).then_inc(consts_ready, 1)

            def inverse_std(kind, t, n_before, n_own):
                pool.wait_ge(ln_stats, n_before + 1)
                passed("pool", pool)
                pool.tensor_scalar(veps[:, kind, t:t + 1], mv[:, kind, t, 1:2], EPS, None,
                                   ALU.add).then_inc(pool_step, 1)
                pool.wait_ge(pool_step, n_own)
                pool.tensor_tensor(rstd[:, kind, t:t + 1], veps[:, kind, t:t + 1], minus_half[:, :],
                                   ALU.pow).then_inc(ln_rstd, 1)

            consts = pools[0]
            for t in range(NT):
                inverse_std(0, t, t, consts + t + 1)

            def send_places(n):
                pool.wait_ge(place_ready, n + 1)
                passed("pool", pool)
                for t in range(NT):
                    pool.indirect_dma_start(out=perm, out_offset=bass.IndirectOffsetOnAxis(ap=place_i[:, t:t + 1], axis=0),
                                            in_=tok_id[:, t:t + 1], in_offset=None).then_inc(lists_sent, 16)

            pool.wait_ge(inits_out, 32)
            def body(b, last):
                lns = NT + b * 2 * NT
                for s in range(NU + 1):
                    if s < NU:
                        q, g, t0, n = unit(s)
                        sc = probs[0:n, s % 3, 0:HQ * n].rearrange("p (h n) -> p h n", n=n)
                        pool.wait_ge(top_ready, NU * b + s + 1)
                        pool.tensor_tensor(sc, sc, top[0:n, s % 3, :].unsqueeze(2).to_broadcast([n, HQ, n]),
                                           ALU.subtract).then_inc(shifted, 1)
                    if s >= 1:
                        q, g, t0, n = unit(s - 1)
                        sc = probs[0:n, (s - 1) % 3, 0:HQ * n].rearrange("p (h n) -> p h n", n=n)
                        pool.wait_ge(share_ready, NU * b + s)
                        pool.tensor_tensor(sc, sc, share[0:n, (s - 1) % 3, :].unsqueeze(2).to_broadcast([n, HQ, n]),
                                           ALU.mult).then_inc(probs_ready, 1)
                    if s == 2:
                        pool.wait_ge(xn_ready, NT * b + NT)
                        pool.wait_ge(rows_ready, NT * b + 1)
                        passed("pool", pool)
                        pool.tensor_copy(hres[:, :, :], h[:, :, :]).then_inc(hres_ready, 1)
                    if s == 3:
                        send_places(b)
                    if 6 <= s < 9 and not last:
                        inverse_std(0, s - 6, lns + s - 6, consts + lns + s - 6 + 1)
                after = lns + (0 if last else NT)
                for t in range(NT):
                    inverse_std(1, t, after + t, consts + after + t + 1)

            with pool.Fori(0, NB - 1) as b:
                body(b, False)
            body(NB - 1, True)
            send_places(NB)

            def gather(j):
                pool.wait_ge(ids_here[j], 16)
                if j >= 4:
                    pool.wait_ge(res_ready, j - 3)
                pool.indirect_dma_start(out=xg[j % 4], out_offset=None, in_=table,
                                        in_offset=bass.IndirectOffsetOnAxis(ap=ids[:, j:j + 1], axis=0)
                                        ).then_inc(xg_here[j % 4], 16)

            for j in range(4):
                gather(j)
            for j in range(FFT):
                if j + 4 < FFT:
                    gather(j + 4)
                pool.wait_ge(y_ready, j + 2)
                pool.indirect_dma_start(out=out, out_offset=bass.IndirectOffsetOnAxis(ap=ids[:, j:j + 1], axis=0),
                                        in_=yo[j % 4], in_offset=None, bounds_check=TOKENS - 1,
                                        oob_is_err=False).then_inc(out_sent[j % 4], 16)
                if j >= 2:
                    pool.wait_ge(out_sent[(j - 2) % 4], 16 * ((j - 2) // 4 + 1))
                    pool.sem_inc(yo_free, 1)
            for j in (FFT - 2, FFT - 1):
                pool.wait_ge(out_sent[j % 4], 16 * (j // 4 + 1))


OWN_PER_BLOCK = NU + 2 * NT + 2 + 1 + 1 + 3


def kernel(x, L0_tok_W_repr, L0_tok_b_repr, L0_tok_W_proj, L0_tok_b_proj, L0_attn_W_qkv, L0_attn_W_out,
           L0_ffn_gate_w, L0_ffn_gate_b, L0_ffn_w1, L0_ffn_b1, L0_ffn_w2, L0_ffn_b2):
    from concourse import bacc
    from concourse.bass_utils import run_bass_kernel_spmd

    half = PATCH // 2
    per = IMAGES // NB
    arrays = {
        "xT": np.asarray(x).reshape(NB, per, CHANNELS, GRID, 2, half, GRID, PATCH)
        .transpose(0, 5, 7, 2, 4, 1, 3, 6).reshape(NB, P, KX, BT),
        "w_proj": np.asarray(L0_tok_W_proj).reshape(REPR, D, 2, P).transpose(3, 2, 0, 1),
        "w_repr": np.asarray(L0_tok_W_repr).reshape(REPR * CHANNELS),
        "b_repr": np.asarray(L0_tok_b_repr),
        "b_proj": np.asarray(L0_tok_b_proj),
        "w_qkv": np.asarray(L0_attn_W_qkv).T,
        "w_out": np.asarray(L0_attn_W_out).T.reshape(PAIRS, P, D).transpose(1, 0, 2),
        "gate_w": np.asarray(L0_ffn_gate_w),
        "gate_b": np.asarray(L0_ffn_gate_b).reshape(1, EXPERTS),
        "w1": np.asarray(L0_ffn_w1).transpose(1, 0, 2),
        "b1": np.asarray(L0_ffn_b1).reshape(1, EXPERTS, FF),
        "w2": np.asarray(L0_ffn_w2).reshape(EXPERTS, FCH, P, D).transpose(2, 0, 1, 3),
        "b2": np.asarray(L0_ffn_b2),
    }
    nc = bacc.Bacc("TRN2", target_bir_lowering=False, num_devices=1)
    args = []
    for name in arrays:
        arrays[name] = np.ascontiguousarray(arrays[name])
        args.append(nc.dram_tensor(name, arrays[name].shape, F32, kind="ExternalInput").ap())
    args.append(nc.dram_tensor("out", [TOKENS, D], F32, kind="ExternalOutput").ap())
    build(nc, *args)
    r = run_bass_kernel_spmd(nc, [arrays], core_ids=[0])
    return r.results[0]["out"].reshape(IMAGES, PER_IMAGE, D)
```

```python
from contextlib import ExitStack

import numpy as np

import concourse.bass as bass
from concourse import mybir

ALU = mybir.AluOpType
ACT = mybir.ActivationFunctionType
AX = mybir.AxisListType
F32 = mybir.dt.float32
F32R = mybir.dt.float32r
BF16 = mybir.dt.bfloat16
U32 = mybir.dt.uint32
I32 = mybir.dt.int32

IMAGES, CHANNELS, SIDE, PATCH = 32, 3, 96, 16
GRID = SIDE // PATCH
PER_IMAGE = GRID * GRID
TOKENS = IMAGES * PER_IMAGE
REPR, D = 5, 192
HEADS, DH = 12, 64
HD = HEADS * DH
EXPERTS, FF = 8, 768
P = 128

NB = 4
BT = TOKENS // NB
TT = 96
NT = BT // TT
KX = CHANNELS * PATCH * PATCH // P
DA, DB = 128, 64
PAIRS = HEADS // 2
GROUPS = [(0, 108), (108, 108), (216, 72)]
GMAX = 108
HQ = 4
UNITS = [(q, g) for q in range(HEADS // HQ) for g in range(len(GROUPS))]
NU = len(UNITS)
LAG_T, LAG_AV = 2, 3
EPS = 1e-5
LOGIT_SCALE = 8.0
MASKED = -1.0e30

SLOT = 128
FFT = (TOKENS + EXPERTS * (SLOT - 1)) // SLOT
FCH = FF // P
SPARE_ROW = TOKENS
LISTS = EXPERTS * TOKENS
SPARE_SLOTS = 3 * P
PERM_COLS = (LISTS + SPARE_SLOTS) // P

W1_PIECE = EXPERTS * FF // (NB - 1)

WQ_PIECES = [slice(0, HD + HQ * DH), slice(HD + HQ * DH, 3 * HD)]

ACC = [0, 1, 2, 3]
SC_BANK, TR_BANK, AV_BANK = 4, 5, 6


def per_block_products(last):
    order = []
    for s in range(2 * len(GROUPS)):
        order += step_products(s)
    if not last:
        order += [("tok", t) for t in range(NT)]
        order += [("xt", t) for t in range(NT)] + [("q", 0), ("k", 0)]
    order += [("o", t) for t in range(NT)]
    if not last:
        order += [("q", 1), ("k", 1)]
        order += [("gt", 0), ("v", 0, 0), ("gt", 1), ("v", 0, 1), ("gt", 2), ("v", 1, 0), ("v", 1, 1),
                  ("lg",), ("v", 2, 0), ("v", 2, 1), ("rk",)]
    else:
        order += [("gt", 0), ("gt", 1), ("gt", 2), ("lg",), ("rk",)]
    return order


def step_products(s):
    c = 2 * (s // 3 + 1)
    return [[("q", c), ("k", c)], [("q", c + 1)], [("k", c + 1)]][s % 3]


OPENING = ([("tok", 0), ("bias",), ("tok", 1), ("tok", 2)] + [("xt", t) for t in range(NT)]
           + [("q", 0), ("k", 0), ("q", 1), ("k", 1)] + [("v", g, f) for g in range(3) for f in range(2)])
MIDDLE, FINAL = per_block_products(False), per_block_products(True)
assert len(MIDDLE) % len(ACC) == 0


def product(key, b, opening=False):
    if opening:
        n, blocks = OPENING.index(key), 0
    elif isinstance(b, int) and b == NB - 1:
        n, blocks = len(OPENING) + FINAL.index(key), b
    else:
        n, blocks = len(OPENING) + MIDDLE.index(key), b
    return n % len(ACC), n // len(ACC) + blocks * (len(MIDDLE) // len(ACC))


def build(nc, xT, w_proj, w_repr, b_repr, b_proj, w_qkv, w_out, gate_w, gate_b, w1, b1, w2, b2, out):
    table = nc.dram_tensor("token_table", [TOKENS + 1, 2 * D], F32, kind="Internal").ap()
    perm = nc.dram_tensor("expert_lists", [LISTS + SPARE_SLOTS, 1], U32, kind="Internal").ap()

    with ExitStack() as ctx:
        def sb(name, shape, dt=F32):
            return ctx.enter_context(nc.sbuf_tensor(name, shape, dt))

        def sb_shared(*tensors):
            handles = []
            for i, (name, shape, dt) in enumerate(tensors):
                if i < len(tensors) - 1:
                    with nc.sbuf_tensor(name, shape, dt) as t:
                        handles.append(t)
                else:
                    handles.append(sb(name, shape, dt))
            return handles

        def sem(name):
            return ctx.enter_context(nc.semaphore(name))

        psum = ctx.enter_context(nc.psum_tensor("psum", [P, 8, 512], F32))

        wr = sb("wr", [P, REPR * CHANNELS])
        br = sb("br", [P, REPR])
        bp = sb("bp", [REPR, D])
        late = sb("late", [P, EXPERTS * FF])
        b1s = late[:, :].rearrange("p (e f) -> p e f", e=EXPERTS)
        v_cols, p_cols = len(GROUPS) * HD, 3 * HQ * GMAX
        v = late[:, 0:v_cols].rearrange("p (g c) -> p g c", g=len(GROUPS))
        probs = late[0:GMAX, v_cols:v_cols + p_cols].rearrange("p (s n) -> p s n", s=3)
        probsT = late[0:GMAX, v_cols + p_cols:v_cols + 2 * p_cols].rearrange("p (s n) -> p s n", s=3)
        w_first = v_cols + 2 * p_cols
        weff = late[:, w_first:w_first + 2 * CHANNELS * D].rearrange("p (c h e) -> p c h e", c=CHANNELS, h=2)
        wb = sb("wb", [P, 2, D])
        bias = sb("bias", [TT, D])
        w2s, wq_in, wq_parts = sb_shared(("w2s", [P, EXPERTS, FCH, D], F32), ("wq_in", [P, 4, 3 * HD], F32),
                                         ("wq_parts", [P, 4, 3 * HD], F32R))
        wqA_hi, wqA_lo, wqB = [wq_parts[:, i, :] for i in range(3)]
        wqA_in, wqB_in = wq_in[:, 1, :], wq_in[:, 3, :]
        wo = sb("wo", [P, PAIRS, D])
        gwA = sb("gwA", [DA, EXPERTS])
        gwB = sb("gwB", [DB + 1, EXPERTS])
        w1A_hi = sb("w1A_hi", [DA, EXPERTS * FF], F32R)
        w1A_in, w1A_lo = sb_shared(("w1A_in", [DA, EXPERTS * FF], F32), ("w1A_lo", [DA, EXPERTS * FF], F32R))
        wp_last = w1A_in[:, 0:2 * REPR * D].rearrange("p (r h e) -> p r h e", r=REPR, h=2)
        w1B_in, w1B = sb_shared(("w1B_in", [2 * DB, EXPERTS * FF], F32), ("w1B", [2 * DB, EXPERTS * FF], F32R))
        w1B_part = sb("w1B_part", [DB, W1_PIECE], F32R)
        ident = sb("ident", [P, P])
        ones = sb("ones", [P, TT])
        mask = sb("mask", [GMAX, GMAX])
        before = sb("before", [TT, TT], BF16)
        all1 = sb("all1", [TT, TT], BF16)
        minus_half = sb("minus_half", [TT, 1])
        iota_i = sb("iota_i", [TT, 16], I32)
        iota = sb("iota", [TT, 16])
        tok_i = sb("tok_i", [TT, NT], I32)
        tok_f = sb("tok_f", [TT, NT])
        xb = sb("xb", [P, KX, BT])
        h = sb("h", [TT, NT, D])
        hres = sb("hres", [TT, NT, D])
        xn_hi = sb("xn_hi", [P, 2, BT], F32R)
        xnA_lo = sb("xnA_lo", [DA, BT], F32R)
        xnB_lo2 = sb("xnB_lo2", [2 * DB, BT], F32R)
        xnB_lo = xnB_lo2[0:DB, :]
        xnA_hi, xnB = xn_hi[:, 0, :], xn_hi[:, 1, :]
        qT = sb("qT", [P, PAIRS, BT])
        kT = sb("kT", [P, PAIRS, 2, BT])
        wp = late[:, 0:2 * REPR * D].rearrange("p (h r e) -> p h r e", h=2, r=REPR)
        oT = sb("oT", [P, PAIRS, BT])
        top = sb("top", [GMAX, 3, HQ])
        total = sb("total", [GMAX, 3, HQ])
        share = sb("share", [GMAX, 3, HQ])
        rows = sb("rows", [TT, NT, 2 * D])
        xn = rows[:, :, D:2 * D]
        xn2A = sb("xn2A", [DA, BT])
        xn2B = sb("xn2B", [DB + 1, BT])
        stats = sb("stats", [TT, 2, NT, 6])
        mv = sb("mv", [TT, 2, NT, 2])
        veps = sb("veps", [TT, 2, NT])
        rstd = sb("rstd", [TT, 2, NT])
        lg = sb("lg", [TT, NT, EXPERTS])
        lgmax = sb("lgmax", [TT, NT, 8])
        lgidx = sb("lgidx", [TT, NT, 8], U32)
        chosen = sb("chosen", [TT, NT])
        onehot = sb("onehot", [TT, NT, EXPERTS], BF16)
        place = sb("place", [TT, NT, EXPERTS])
        place_f = sb("place_f", [TT, NT])
        place_i = sb("place_i", [TT, NT], U32)
        tok_id = sb("tok_id", [TT, NT], U32)
        filled = sb("filled", [TT, EXPERTS])
        steps9 = sb("steps9", [1, EXPERTS, 9])
        cnt = sb("cnt", [1, EXPERTS])
        ntile = sb("ntile", [1, EXPERTS])
        tend = sb("tend", [1, EXPERTS])
        off = sb("off", [1, EXPERTS])
        grid = sb("grid", [1, FFT, EXPERTS])
        grid2 = sb("grid2", [1, FFT, EXPERTS])
        te = sb("te", [1, FFT])
        te7 = sb("te7", [1, FFT])
        tr = sb("tr", [1, FFT])
        tr2 = sb("tr2", [1, FFT])
        tile_expert = sb("tile_expert", [1, FFT], I32)
        tile_row = sb("tile_row", [1, FFT], I32)
        ids = sb("ids", [SLOT, FFT], U32)
        zeros = sb("zeros", [1, 2 * D])
        spare = sb("spare", [P, PERM_COLS], U32)
        xbf = xb[:, :, :].rearrange("p k n -> p (k n)")
        xg = [xbf[:, i * 2 * D:(i + 1) * 2 * D] for i in range(4)]
        fxA_hi, fxA_lo, fxB, fxB_lo = [[w[:, i * SLOT:(i + 1) * SLOT] for i in range(2)]
                                       for w in (xnA_hi, xnA_lo, xnB, xnB_lo2[:, :])]
        qTf = qT[:, :, :].rearrange("p k n -> p (k n)")
        kTf = kT[:, :, :, :].rearrange("p k i n -> p (k i n)")
        oTf = oT[:, :, :].rearrange("p k n -> p (k n)")
        hid = [qTf[:, 0:FF], qTf[:, FF:2 * FF]]
        hidT = [kTf[:, 0:FF], kTf[:, FF:2 * FF]]
        b2s = kTf[:, 2 * FF:2 * FF + EXPERTS * D].rearrange("p (e d) -> p e d", e=EXPERTS)
        res = [oTf[:, i * D:(i + 1) * D] for i in range(4)]
        yo = [oTf[:, (4 + i) * D:(5 + i) * D] for i in range(4)]

        x_here = sem("x_here")
        wp_here = sem("wp_here")
        br_here = sem("br_here")
        wq_here = [sem(f"wq_here{i}") for i in range(len(WQ_PIECES))]
        wq_hi_ready = sem("wq_hi_ready")
        w1_here = sem("w1_here")
        w1_hi_ready = sem("w1_hi_ready")
        w1A_split, w1_split = sem("w1A_split"), sem("w1_split")
        wq_split = sem("wq_split")
        wo_here = sem("wo_here")
        w2_here = sem("w2_here")
        b1_here = sem("b1_here")
        b2_here = sem("b2_here")
        inits_out = sem("inits_out")
        full = [sem(f"acc_full{i}") for i in ACC]
        free = [sem(f"acc_free{i}") for i in ACC]
        sc_full, sc_free = sem("sc_full"), sem("sc_free")
        tr_full, tr_free = sem("tr_full"), sem("tr_free")
        av_full, av_free = sem("av_full"), sem("av_free")
        top_ready = sem("top_ready")
        exp_ready = sem("exp_ready")
        probs_ready = sem("probs_ready")
        ln_stats = sem("ln_stats")
        ln_rstd = sem("ln_rstd")
        xn_ready = sem("xn_ready")
        xn_hi_ready = sem("xn_hi_ready")
        rows_ready = sem("rows_ready")
        hres_ready = sem("hres_ready")
        onehot_ready = sem("onehot_ready")
        place_ready = sem("place_ready")
        rows_sent = sem("rows_sent")
        lists_sent = sem("lists_sent")
        dve_step = sem("dve_step")
        pool_step = sem("pool_step")
        waited = {"dve": sem("dve_waited"), "pool": sem("pool_waited")}
        ident_ready = sem("ident_ready")
        consts_ready = sem("consts_ready")
        weff_ready = sem("weff_ready")
        scaled = sem("scaled")
        wb_ready = sem("wb_ready")
        kt_zero = sem("kt_zero")
        tiles_ready = sem("tiles_ready")
        ids_here = [sem(f"ids_here{j}") for j in range(FFT)]
        xg_here = [sem(f"xg_here{i}") for i in range(4)]
        fxt_full, fx_hi_ready, fx_ready = sem("fxt_full"), sem("fx_hi_ready"), sem("fx_ready")
        up_full, biased, hid_ready = sem("up_full"), sem("biased"), sem("hid_ready")
        hidt_full, hidt_ready = sem("hidt_full"), sem("hidt_ready")
        down_full, y_ready = sem("down_full"), sem("y_ready")
        res_ready = sem("res_ready")
        yo_free = sem("yo_free")
        out_sent = [sem(f"out_sent{i}") for i in range(4)]

        def acc(bank):
            return psum[:, ACC[bank], :]

        def taken(eng, slot):
            bank, before_it = slot
            eng.wait_ge(free[bank], before_it + 1)

        def all_taken(eng, keys, b, opening=False, following=None):
            last = {}
            for key in keys:
                last[product(key, b, opening)[0]] = product(key, b, opening)
            for bank, slot in last.items():
                if following is None or bank != following[0]:
                    taken(eng, slot)

        def complete(eng, slot):
            bank, before_it = slot
            eng.wait_ge(full[bank], before_it + 1)

        def passed(name, eng):
            eng.sem_inc(waited[name], 1)

        def unit(u):
            q, g = UNITS[u]
            return (q, g) + GROUPS[g]

        block = ctx.enter_context(nc.Block())

        @block.sync
        def _(sp):
            sp.sem_inc(rows_sent, 16)
            sp.dma_start(wr[:, :], w_repr.partition_broadcast(P)).then_inc(wp_here, 16)
            sp.dma_start(wp, w_proj).then_inc(wp_here, 16)
            sp.dma_start(xb[:, :, :], xT[0]).then_inc(x_here, 16)
            sp.dma_start(br[:, :], b_repr.partition_broadcast(P)).then_inc(br_here, 16)
            sp.dma_start(bp[:, :], b_proj).then_inc(br_here, 16)
            for i, cols in enumerate(WQ_PIECES):
                sp.dma_start(wqA_in[:, cols], w_qkv[0:DA, cols]).then_inc(wq_here[i], 16)
                sp.dma_start(wqB_in[0:DB, cols], w_qkv[DA:D, cols]).then_inc(wq_here[i], 16)
            sp.dma_start(wo[:, :, :], w_out).then_inc(wo_here, 16)
            sp.dma_start(gwA[:, :], gate_w[0:DA, :]).then_inc(wo_here, 16)
            sp.dma_start(gwB[0:DB, :], gate_w[DA:D, :]).then_inc(wo_here, 16)
            sp.dma_start(gwB[DB:DB + 1, :], gate_b).then_inc(wo_here, 16)
            sp.wait_ge(consts_ready, 1)
            sp.dma_start(perm.rearrange("(p c) o -> p (c o)", c=PERM_COLS), spare[:, :]).then_inc(inits_out, 16)
            sp.dma_start(table[SPARE_ROW:SPARE_ROW + 1, :], zeros[:, :]).then_inc(inits_out, 16)

            def body(b, last):
                if not last:
                    sp.wait_ge(xn_ready, NT * b + NT)
                    sp.dma_start(xb[:, :, :], xT[b + 1]).then_inc(x_here, 16)
                sp.wait_ge(rows_ready, NT * b + NT + 1)
                sp.dma_start(table[bass.ds(b * BT, BT), :].rearrange("(t p) d -> p t d", p=TT),
                             rows[:, :, :]).then_inc(rows_sent, 16)

            with sp.Fori(0, NB - 1) as b:
                body(b, False)
            complete(sp, product(("k", PAIRS - 1), NB - 1))
            sp.dma_start(w2s[:, :, :, :], w2).then_inc(w2_here, 16)
            sp.wait_ge(sc_full, NU * NB)
            sp.dma_start(b2s, b2.partition_broadcast(P)).then_inc(b2_here, 16)
            sp.wait_ge(av_full, NU * NB)
            sp.dma_start(b1s[:, 0:EXPERTS // 2, :], b1[0:EXPERTS // 2].partition_broadcast(P)).then_inc(b1_here, 16)
            body(NB - 1, True)
            sp.dma_start(b1s[:, EXPERTS // 2:, :], b1[EXPERTS // 2:].partition_broadcast(P)).then_inc(b1_here, 16)

            sp.wait_ge(rows_sent, 16 * NB + 16)
            sp.wait_ge(lists_sent, 16 * NT * (NB + 1))
            sp.wait_ge(tiles_ready, 1)
            for j in range(FFT):
                row = sp.value_load(tile_row[0:1, j:j + 1], min_val=0, max_val=LISTS)
                sp.dma_start(ids[:, j:j + 1], perm[bass.ds(row, SLOT), :]).then_inc(ids_here[j], 16)

        @block.tensor
        def _(pe):
            def into(slot):
                bank, before_it = slot
                pe.wait_ge(free[bank], before_it)
                return acc(bank)

            def tokens(t, slot):
                dst = into(slot)
                for k in range(KX):
                    mm = pe.matmul(dst[0:TT, 0:D], xb[:, k, t * TT:(t + 1) * TT], weff[:, k // 2, k % 2, :],
                                   start=(k == 0), stop=(k == KX - 1))
                mm.then_inc(full[slot[0]], 1)

            def turn_xn(t, slot, ready, src, col):
                dst = into(slot)
                pe.wait_ge(*ready)
                pe.transpose(dst[0:DA, 0:TT], src[:, t, col:col + DA], ident[0:TT, 0:TT])
                pe.transpose(dst[0:DB, TT:2 * TT], src[:, t, col + DA:col + D],
                             ident[0:TT, 0:TT]).then_inc(full[slot[0]], 1)

            def split_product(dst, parts):
                for i, (lhsT, rhs) in enumerate(parts):
                    mm = pe.matmul(dst, lhsT, rhs, start=(i == 0), stop=(i == len(parts) - 1))
                return mm

            def heads(which, c, slot):
                dst = into(slot)
                col = (0 if which == "q" else HD) + c * P
                cs = slice(col, col + P)
                split_product(dst[:, 0:BT], [
                    (wqA_hi[:, cs], xnA_hi), (wqA_hi[:, cs], xnA_lo[:, :]), (wqA_lo[:, cs], xnA_hi),
                    (wqB[:, cs], xnB), (wqB[0:DB, cs], xnB_lo)]).then_inc(full[slot[0]], 1)

            def values(g, f, slot):
                dst = into(slot)
                t0, n = GROUPS[g]
                col = 2 * HD + f * (HD // 2)
                ts, cs = slice(t0, t0 + n), slice(col, col + HD // 2)
                split_product(dst[0:n, 0:HD // 2], [
                    (xnA_hi[:, ts], wqA_hi[:, cs]), (xnA_lo[:, ts], wqA_hi[:, cs]), (xnA_hi[:, ts], wqA_lo[:, cs]),
                    (xnB[:, ts], wqB[:, cs]), (xnB_lo[:, ts], wqB[0:DB, cs])]).then_inc(full[slot[0]], 1)

            def scores(u, b):
                q, g, t0, n = unit(u)
                pe.wait_ge(sc_free, NU * b + u + 1)
                for i in range(2):
                    c = 2 * q + i
                    mm = pe.matmul(psum[0:n, SC_BANK, 2 * i * n:2 * (i + 1) * n].rearrange("p (i n) -> p i n", i=2), qT[:, c, t0:t0 + n],
                                   kT[:, c, :, t0:t0 + n], start=True, stop=True)
                mm.then_inc(sc_full, 1)

            def turn_probs(u, b):
                q, g, t0, n = unit(u)
                pe.wait_ge(probs_ready, NU * b + u + 1)
                pe.wait_ge(tr_free, NU * b + u + 1)
                for i in range(HQ):
                    mm = pe.transpose(psum[0:n, TR_BANK, i * n:(i + 1) * n], probs[0:n, u % 3, i * n:(i + 1) * n],
                                      ident[0:n, 0:n])
                mm.then_inc(tr_full, 1)

            def attend(u, b):
                q, g, t0, n = unit(u)
                pe.wait_ge(tr_free, NU * b + u + 2)
                pe.wait_ge(av_free, NU * b + u + 1)
                for i in range(2):
                    c = 2 * q + i
                    mm = pe.matmul(psum[:, AV_BANK, 2 * i * n:2 * (i + 1) * n], v[0:n, g, c * P:(c + 1) * P],
                                   probsT[0:n, u % 3, 2 * i * n:2 * (i + 1) * n], start=True, stop=True)
                mm.then_inc(av_full, 1)

            def project(t, slot, b, c0=0, c1=PAIRS):
                dst = into(slot) if c0 == 0 else acc(slot[0])
                pe.wait_ge(av_free, NU * b + NU * c1 // PAIRS + 1)
                for c in range(c0, c1):
                    mm = pe.matmul(dst[0:TT, 0:D], oT[:, c, t * TT:(t + 1) * TT], wo[:, c, :],
                                   start=(c == 0), stop=(c == PAIRS - 1))
                if c1 == PAIRS:
                    mm.then_inc(full[slot[0]], 1)

            def gate(b):
                slot = product(("lg",), b)
                all_taken(pe, [("gt", t) for t in range(NT)], b, following=slot)
                dst = into(slot)
                for t in range(NT):
                    pe.matmul(dst[0:TT, t * EXPERTS:(t + 1) * EXPERTS], xn2A[:, t * TT:(t + 1) * TT], gwA[:, :],
                              start=True, stop=False)
                    mm = pe.matmul(dst[0:TT, t * EXPERTS:(t + 1) * EXPERTS], xn2B[:, t * TT:(t + 1) * TT], gwB[:, :],
                                   start=False, stop=True)
                mm.then_inc(full[slot[0]], 1)

            def ranks(b):
                slot = product(("rk",), b)
                dst = into(slot)
                pe.wait_ge(onehot_ready, b + 1)
                for t in range(NT):
                    col = t * EXPERTS
                    for e in range(t):
                        pe.matmul(dst[0:TT, col:col + EXPERTS], all1[:, :], onehot[:, e, :],
                                  start=(e == 0), stop=False)
                    pe.matmul(dst[0:TT, col:col + EXPERTS], before[:, :], onehot[:, t, :], start=(t == 0), stop=True)
                col = NT * EXPERTS
                for t in range(NT):
                    mm = pe.matmul(dst[0:TT, col:col + EXPERTS], all1[:, :], onehot[:, t, :],
                                   start=(t == 0), stop=(t == NT - 1))
                mm.then_inc(full[slot[0]], 1)

            def keep_clock(n):
                for _ in range(n):
                    pe.transpose(psum[:, TR_BANK, 0:P], ident[:, :], ident[:, :])

            pe.wait_ge(ident_ready, 1)
            pe.wait_ge(wp_here, 32)
            keep_clock(32)
            pe.wait_ge(x_here, 16)
            pe.wait_ge(weff_ready, 2)
            tokens(0, product(("tok", 0), 0, opening=True))
            pe.wait_ge(br_here, 32)
            pe.wait_ge(wb_ready, 1)
            slot = product(("bias",), 0, opening=True)
            dst = into(slot)
            pe.matmul(dst[0:TT, 0:D], ones[:, :], wb[:, 0, :], start=True, stop=False)
            pe.matmul(dst[0:TT, 0:D], ones[:, :], wb[:, 1, :], start=False, stop=False)
            pe.matmul(dst[0:TT, 0:D], ones[0:REPR, :], bp[:, :], start=False, stop=True).then_inc(full[slot[0]], 1)
            for t in range(1, NT):
                tokens(t, product(("tok", t), 0, opening=True))
            for t in range(NT):
                turn_xn(t, product(("xt", t), 0, opening=True), (xn_ready, t + 1), xn, 0)
            pe.wait_ge(wq_hi_ready, 2)
            pe.wait_ge(wq_split, 2)
            all_taken(pe, [("xt", t) for t in range(NT)], 0, opening=True)
            for c in range(2):
                heads("q", c, product(("q", c), 0, opening=True))
                heads("k", c, product(("k", c), 0, opening=True))
            pe.wait_ge(wq_hi_ready, 4)
            pe.wait_ge(wq_split, 4)
            for g in range(3):
                for f in range(2):
                    values(g, f, product(("v", g, f), 0, opening=True))

            def start_taken(b, opening):
                all_taken(pe, [(w, c) for c in range(2) for w in "qk"] +
                          [("v", g, f) for g in range(3) for f in range(2)], b, opening)

            def body(b, last):
                for s in range(NU + LAG_AV):
                    if s < NU:
                        if s in (3, 6):
                            all_taken(pe, [(w, c) for c in (2 * (s // 3), 2 * (s // 3) + 1) for w in "qk"], b)
                        scores(s, b)
                    if s < 6:
                        for w, c in step_products(s):
                            heads(w, c, product((w, c), b))
                    elif s < 9 and not last:
                        if s == 6:
                            pe.wait_ge(x_here, 16 * b + 32)
                        tokens(s - 6, product(("tok", s - 6), b))
                    if LAG_T <= s < NU + LAG_T:
                        turn_probs(s - LAG_T, b)
                    if s >= LAG_AV:
                        attend(s - LAG_AV, b)
                    if s >= 9 and not last:
                        for t in [[0, 1], [2], []][s - 9]:
                            turn_xn(t, product(("xt", t), b), (xn_ready, NT * b + NT + t + 1), xn, 0)
                        if s == 10:
                            slot = product(("q", 0), b)
                            all_taken(pe, [("xt", t) for t in range(NT)], b, following=slot)
                            heads("q", 0, slot)
                        if s == 11:
                            heads("k", 0, product(("k", 0), b))
                    elif s >= 9:
                        project(s - 9, product(("o", s - 9), b), b, 0, PAIRS - 2)
                for t in range(NT):
                    project(t, product(("o", t), b), b, PAIRS - 2 if last else 0)
                if not last:
                    heads("q", 1, product(("q", 1), b))
                    heads("k", 1, product(("k", 1), b))
                for t in range(NT):
                    turn_xn(t, product(("gt", t), b), (rows_ready, NT * b + t + 2), rows, D)
                    if not last:
                        for g, f in [[(0, 0)], [(0, 1)], [(1, 0), (1, 1)]][t]:
                            values(g, f, product(("v", g, f), b))
                gate(b)
                if not last:
                    values(2, 0, product(("v", 2, 0), b))
                    values(2, 1, product(("v", 2, 1), b))
                ranks(b)
                if not last:
                    start_taken(b, False)

            start_taken(0, True)
            pe.wait_ge(wo_here, 64)
            with pe.Fori(0, NB - 1) as b:
                body(b, False)
            body(NB - 1, True)

            def turn_x(r, i):
                j = r * 4 + i
                pe.wait_ge(xg_here[i % 4], r * 16 + 16 * (i // 4 + 1))
                pe.wait_ge(fx_ready, j)
                pe.transpose(psum[0:DA, 7, 0:SLOT], xg[i % 4][:, D:D + DA], ident[:, :])
                pe.transpose(psum[0:DB, 7, SLOT:2 * SLOT], xg[i % 4][:, D + DA:2 * D],
                             ident[:, :]).then_inc(fxt_full, 1)

            def up(r, i):
                j = r * 4 + i
                e = pe.value_load(tile_expert[0:1, bass.ds(j, 1)], min_val=0, max_val=EXPERTS - 1)
                pe.wait_ge(fx_ready, j + 1)
                p2 = i % 2
                for lo, hi in ((0, 512), (512, FF)):
                    wA, wA_lo, wB = [w.rearrange("p (e f) -> p e f", e=EXPERTS)[:, bass.ds(e, 1), lo:hi]
                                     for w in (w1A_hi[:, :], w1A_lo[:, :], w1B[:, :])]
                    split_product(psum[:, 2 * p2 + lo // 512, 0:hi - lo], [
                        (fxA_hi[p2], wA), (fxA_lo[p2], wA), (fxA_hi[p2], wA_lo),
                        (fxB[p2], wB), (fxB_lo[p2], wB)]).then_inc(up_full, 1)

            def turn_hidden(r, i):
                j = r * 4 + i
                pe.wait_ge(hid_ready, j + 1)
                pe.wait_ge(hidt_ready, j + 1)
                for c in range(FCH):
                    mm = pe.transpose(psum[:, 4 + c // 4, (c % 4) * P:(c % 4 + 1) * P],
                                      hid[i % 2][:, c * P:(c + 1) * P], ident[:, :])
                mm.then_inc(hidt_full, 1)

            def down(r, i):
                j = r * 4 + i
                e = pe.value_load(tile_expert[0:1, bass.ds(j, 1)], min_val=0, max_val=EXPERTS - 1)
                pe.wait_ge(hidt_ready, j + 2)
                pe.wait_ge(y_ready, j + 1)
                for c in range(FCH):
                    mm = pe.matmul(psum[:, 6, 0:D], hidT[i % 2][:, c * P:(c + 1) * P],
                                   w2s[:, bass.ds(e, 1), c, :], start=(c == 0), stop=(c == FCH - 1))
                mm.then_inc(down_full, 1)

            pe.wait_ge(tiles_ready, 1)
            pe.wait_ge(w1_split, NB)
            pe.wait_ge(w2_here, 16)
            pe.wait_ge(ids_here[0], 16)
            keep_clock(16)
            turn_x(0, 0)
            up(0, 0)
            turn_x(0, 1)
            up(0, 1)
            turn_x(0, 2)

            def four_tiles(r, last):
                for i in range(4):
                    turn_hidden(r, i)
                    if not last or i < 2:
                        up(r, i + 2)
                    if not last or i < 1:
                        turn_x(r, i + 3)
                    down(r, i)

            with pe.Fori(0, FFT // 4 - 1) as r:
                four_tiles(r, False)
            four_tiles(FFT // 4 - 1, True)

        @block.scalar
        def _(act):
            act.sem_inc(tr_free, 1)
            act.sem_inc(av_free, 1)
            act.wait_ge(wp_here, 32)
            for r in range(REPR):
                s = (r + 1) * CHANNELS - 1
                act.activation(wp_last[:, r, :, :], wp[:, :, r, :], ACT.Identity, scale=wr[:, s:s + 1]).then_inc(scaled, 1)
            for i, cols in enumerate(WQ_PIECES):
                act.wait_ge(wq_here[i], 32)
                act.copy(wqA_hi[:, cols], wqA_in[:, cols]).then_inc(wq_hi_ready, 1)
                act.copy(wqB[0:DB, cols], wqB_in[0:DB, cols]).then_inc(wq_hi_ready, 1)
            act.wait_ge(weff_ready, 2)
            act.dma_start(w1A_in[:, :], w1[0:DA, :]).then_inc(w1_here, 16)
            for i in range(2):
                act.dma_start(w1B_in[i * DB:(i + 1) * DB, :], w1[DA:D, :]).then_inc(w1_here, 16)

            def take_xn_hi(t, slot):
                complete(act, slot)
                ts, src = slice(t * TT, (t + 1) * TT), acc(slot[0])
                act.copy(xnA_hi[:, ts], src[:, 0:TT])
                for i in range(2):
                    cp = act.copy(xnB[i * DB:(i + 1) * DB, ts], src[0:DB, TT:2 * TT])
                cp.then_inc(xn_hi_ready, 1)

            def round_w1(b):
                cols = bass.ds(b * W1_PIECE, W1_PIECE)
                act.wait_ge(w1_split, b + 1)
                act.copy(w1B_part[:, :], w1B_in[0:DB, cols])
                act.copy(w1B[DB:2 * DB, cols], w1B_in[DB:2 * DB, cols])
                act.copy(w1A_hi[:, cols], w1A_in[:, cols]).then_inc(w1_hi_ready, 1)

            def take_q(c, slot):
                complete(act, slot)
                act.copy(qT[:, c, :], acc(slot[0])[:, 0:BT]).then_inc(free[slot[0]], 1)

            def take_k(c, slot):
                complete(act, slot)
                src = acc(slot[0])
                for i in range(2):
                    rows_ = slice(DH * i, DH * (i + 1))
                    cp = act.copy(kT[rows_, c, i, :], src[rows_, 0:BT])
                cp.then_inc(free[slot[0]], 1)

            def take(w, c, slot):
                (take_q if w == "q" else take_k)(c, slot)

            for t in range(NT):
                take_xn_hi(t, product(("xt", t), 0, opening=True))
            act.wait_ge(kt_zero, 1)
            for c in range(2):
                for w in "qk":
                    take(w, c, product((w, c), 0, opening=True))

            def body(b, last):
                for s in range(NU + LAG_AV):
                    if s < 6:
                        for w, c in step_products(s):
                            take(w, c, product((w, c), b))
                    if LAG_T <= s < NU + LAG_T:
                        u = s - LAG_T
                        q, g, t0, n = unit(u)
                        act.wait_ge(tr_full, NU * b + u + 1)
                        act.copy(probsT[0:n, u % 3, 0:HQ * n], psum[0:n, TR_BANK, 0:HQ * n]).then_inc(tr_free, 1)
                    if s >= LAG_AV:
                        u = s - LAG_AV
                        q, g, t0, n = unit(u)
                        act.wait_ge(av_full, NU * b + u + 1)
                        src = psum[:, AV_BANK, 0:HQ * n].rearrange("p (c i n) -> p c i n", c=2, i=2)
                        for i in range(2):
                            rows_ = slice(DH * i, DH * (i + 1))
                            cp = act.copy(oT[rows_, 2 * q:2 * q + 2, t0:t0 + n], src[rows_, :, i, :])
                        cp.then_inc(av_free, 1)
                    if s < NU:
                        q, g, t0, n = unit(s)
                        act.wait_ge(top_ready, NU * b + s + 1)
                        for i in range(HQ):
                            head = probs[0:n, s % 3, i * n:(i + 1) * n]
                            ex = act.activation(head, head, ACT.Exp, bias=top[0:n, s % 3, i:i + 1],
                                                scale=LOGIT_SCALE, accum_out=total[0:n, s % 3, i:i + 1])
                        ex.then_inc(exp_ready, 1)
                    if s == 9 and not last:
                        for t in range(NT):
                            take_xn_hi(t, product(("xt", t), b))
                    if s >= 10 and not last:
                        take("qk"[s - 10], 0, product(("qk"[s - 10], 0), b))
                if not last:
                    round_w1(b)
                    take("q", 1, product(("q", 1), b))
                    take("k", 1, product(("k", 1), b))
                for t in range(NT):
                    slot = product(("gt", t), b)
                    complete(act, slot)
                    act.copy(xn2A[:, t * TT:(t + 1) * TT], acc(slot[0])[:, 0:TT])
                    act.copy(xn2B[0:DB, t * TT:(t + 1) * TT],
                             acc(slot[0])[0:DB, TT:2 * TT]).then_inc(free[slot[0]], 1)

            act.wait_ge(w1_here, 48)
            with act.Fori(0, NB - 1) as b:
                body(b, False)
            body(NB - 1, True)

            def round_x(r, i):
                j = r * 4 + i
                act.wait_ge(fxt_full, j + 1)
                act.copy(fxA_hi[i % 2], psum[0:DA, 7, 0:SLOT])
                for k in range(2):
                    cp = act.copy(fxB[i % 2][k * DB:(k + 1) * DB, :], psum[0:DB, 7, SLOT:2 * SLOT])
                cp.then_inc(fx_hi_ready, 1)

            act.activation(veps[:, 1, 0:1], minus_half[:, :], ACT.Gelu)

            def gelu(r, i):
                j = r * 4 + i
                for k, (lo, hi) in enumerate(((0, 512), (512, FF))):
                    act.wait_ge(biased, 2 * j + k + 1)
                    ge = act.activation(hid[i % 2][:, lo:hi], hid[i % 2][:, lo:hi], ACT.Gelu)
                ge.then_inc(hid_ready, 1)

            round_x(0, 0)
            round_x(0, 1)
            gelu(0, 0)
            round_x(0, 2)
            gelu(0, 1)

            def four_tiles(r, last):
                for i in range(4):
                    if not last or i < 2:
                        gelu(r, i + 2)
                    if not last or i < 1:
                        round_x(r, i + 3)

            with act.Fori(0, FFT // 4 - 1) as r:
                four_tiles(r, False)
            four_tiles(FFT // 4 - 1, True)

        @block.vector
        def _(dve):
            steps = [0, 0]

            def own(ins):
                ins.then_inc(dve_step, 1)
                steps[0] += 1
                dve.wait_ge(dve_step, steps[1] + steps[0])

            def layernorm_stats(src, kind, t, n_before):
                own(dve.bn_stats(stats[:, kind, t, :], src))
                passed("dve", dve)
                dve.bn_aggr(mv[:, kind, t, :], stats[:, kind, t, :]).then_inc(ln_stats, 1)

            def layernorm(dst, src, kind, t, n_before):
                dve.wait_ge(ln_rstd, n_before + 1)
                return dve.tensor_scalar(dst, src, mv[:, kind, t, 0:1], rstd[:, kind, t:t + 1],
                                         ALU.subtract, ALU.mult)

            def take_tokens(t, slot, n_before):
                complete(dve, slot)
                dve.tensor_tensor(h[:, t, :], acc(slot[0])[0:TT, 0:D], bias[:, :], ALU.add).then_inc(free[slot[0]], 1)
                taken(dve, slot)
                layernorm_stats(h[:, t, :], 0, t, n_before)

            def take_xn_lo(t, slot, n_before):
                dve.wait_ge(xn_hi_ready, n_before + 1)
                ts, src = slice(t * TT, (t + 1) * TT), acc(slot[0])
                dve.tensor_tensor(xnA_lo[:, ts], src[:, 0:TT], xnA_hi[:, ts], ALU.subtract)
                dve.tensor_tensor(xnB_lo[:, ts], src[0:DB, TT:2 * TT], xnB[0:DB, ts],
                                  ALU.subtract).then_inc(free[slot[0]], 1)

            def split_wq(i):
                cols = WQ_PIECES[i]
                dve.wait_ge(wq_hi_ready, 2 * i + 1)
                dve.tensor_tensor(wqA_lo[:, cols], wqA_in[:, cols], wqA_hi[:, cols], ALU.subtract).then_inc(wq_split, 1)
                dve.wait_ge(wq_hi_ready, 2 * i + 2)
                dve.tensor_tensor(wqB[DB:2 * DB, cols], wqB_in[0:DB, cols], wqB[0:DB, cols],
                                  ALU.subtract).then_inc(wq_split, 1)

            def take_v(g, f, slot):
                t0, n = GROUPS[g]
                complete(dve, slot)
                dve.tensor_copy(v[0:n, g, f * (HD // 2):(f + 1) * (HD // 2)],
                                acc(slot[0])[0:n, 0:HD // 2]).then_inc(free[slot[0]], 1)

            dve.sem_inc(sc_free, 1)
            dve.sem_inc(rows_ready, 1)
            dve.sem_inc(hidt_ready, 1)
            dve.sem_inc(y_ready, 1)
            dve.memset(xn2B[DB:DB + 1, :], 1.0)
            dve.memset(kT[:, :, :, :], 0.0).then_inc(kt_zero, 1)
            dve.wait_ge(wp_here, 32)
            for r in range(REPR):
                for c in range(CHANNELS - 1):
                    s = r * CHANNELS + c
                    if r == 0:
                        ins = dve.tensor_scalar(weff[:, c, :, :], wp[:, :, r, :], wr[:, s:s + 1], None, ALU.mult)
                    else:
                        ins = dve.scalar_tensor_tensor(weff[:, c, :, :], wp[:, :, r, :], wr[:, s:s + 1],
                                                       weff[:, c, :, :], ALU.mult, ALU.add)
                own(ins)
            dve.engine_nop().then_inc(weff_ready, 1)
            dve.wait_ge(br_here, 32)
            for r in range(REPR):
                if r == 0:
                    ins = dve.tensor_scalar(wb[:, :, :], wp[:, :, r, :], br[:, r:r + 1], None, ALU.mult)
                else:
                    ins = dve.scalar_tensor_tensor(wb[:, :, :], wp[:, :, r, :], br[:, r:r + 1], wb[:, :, :],
                                                   ALU.mult, ALU.add)
                own(ins)
            dve.engine_nop().then_inc(wb_ready, 1)
            split_wq(0)
            slot = product(("bias",), 0, opening=True)
            complete(dve, slot)
            dve.tensor_copy(bias[:, :], acc(slot[0])[0:TT, 0:D]).then_inc(free[slot[0]], 1)
            taken(dve, slot)
            for t in range(NT):
                take_tokens(t, product(("tok", t), 0, opening=True), t)
            for t in range(NT):
                layernorm(xn[:, t, :], h[:, t, :], 0, t, t).then_inc(xn_ready, 1)
            for t in range(NT):
                take_xn_lo(t, product(("xt", t), 0, opening=True), t)
            split_wq(1)
            dve.wait_ge(consts_ready, 1)
            own(dve.tensor_copy(iota[:, :], iota_i[:, :]))
            dve.tensor_scalar(filled[:, :], iota[:, 0:EXPERTS], float(TOKENS), None, ALU.mult)
            own(dve.tensor_copy(tok_f[:, :], tok_i[:, :]))
            for g in range(3):
                for f in range(2):
                    take_v(g, f, product(("v", g, f), 0, opening=True))
            before_blocks = steps[0]

            def body(b, last):
                steps[0] = 0
                steps[1] = before_blocks + b * OWN_PER_BLOCK
                lns = NT + b * 2 * NT

                def normalise(u):
                    q, g, t0, n = unit(u)
                    dve.wait_ge(exp_ready, NU * b + u + 1)
                    own(dve.reciprocal(share[0:n, u % 3, :], total[0:n, u % 3, :]))
                    ex = probs[0:n, u % 3, 0:HQ * n].rearrange("p (h n) -> p h n", n=n)
                    dve.tensor_tensor(ex, ex, share[0:n, u % 3, :].unsqueeze(2).to_broadcast([n, HQ, n]),
                                      ALU.mult).then_inc(probs_ready, 1)

                for s in range(NU + 1):
                    if s < NU:
                        q, g, t0, n = unit(s)
                        dve.wait_ge(sc_full, NU * b + s + 1)
                        sc = probs[0:n, s % 3, 0:HQ * n].rearrange("p (h n) -> p h n", n=n)
                        dve.tensor_tensor(sc, psum[0:n, SC_BANK, 0:HQ * n].rearrange("p (h n) -> p h n", n=n),
                                          mask[0:n, 0:n].unsqueeze(1).to_broadcast([n, HQ, n]),
                                          ALU.add).then_inc(sc_free, 1)
                        dve.wait_ge(sc_free, NU * b + s + 2)
                        own(dve.tensor_reduce(top[0:n, s % 3, :], sc, AX.X, ALU.max))
                        dve.tensor_scalar(top[0:n, s % 3, :], top[0:n, s % 3, :], -LOGIT_SCALE, None,
                                          ALU.mult).then_inc(top_ready, 1)
                    if s >= 1:
                        normalise(s - 1)
                    if not last:
                        if 7 <= s:
                            t = s - 7
                            if t == 0:
                                dve.wait_ge(rows_sent, 16 * b + 16)
                            layernorm(xn[:, t, :], h[:, t, :], 0, t, lns + t).then_inc(xn_ready, 1)
                        if 6 <= s < 9:
                            if s == 6:
                                dve.wait_ge(hres_ready, b + 1)
                            take_tokens(s - 6, product(("tok", s - 6), b), lns + s - 6)
                        if s == 9:
                            for t in range(NT):
                                take_xn_lo(t, product(("xt", t), b), NT * b + NT + t)
                if last:
                    lns -= NT
                if last:
                    dve.wait_ge(hres_ready, NB)
                    dve.wait_ge(rows_sent, 16 * b + 16)
                for t in range(NT + 1):
                    if t < NT:
                        slot = product(("o", t), b)
                        complete(dve, slot)
                        dve.tensor_tensor(rows[:, t, 0:D], acc(slot[0])[0:TT, 0:D], hres[:, t, :],
                                          ALU.add).then_inc(free[slot[0]], 1)
                        taken(dve, slot)
                        layernorm_stats(rows[:, t, 0:D], 1, t, lns + NT + t)
                    if t >= 1:
                        layernorm(rows[:, t - 1, D:2 * D], rows[:, t - 1, 0:D], 1, t - 1,
                                  lns + NT + t - 1).then_inc(rows_ready, 1)
                if not last:
                    for g, f in ((0, 0), (0, 1), (1, 0), (1, 1)):
                        take_v(g, f, product(("v", g, f), b))
                slot = product(("lg",), b)
                complete(dve, slot)
                dve.tensor_copy(lg[:, :, :].rearrange("p t e -> p (t e)"),
                                acc(slot[0])[0:TT, 0:NT * EXPERTS]).then_inc(free[slot[0]], 1)
                taken(dve, slot)
                passed("dve", dve)
                for t in range(NT):
                    ins = dve.max(lgmax[:, t, :], lg[:, t, :])
                own(ins)
                passed("dve", dve)
                for t in range(NT):
                    ins = dve.max_index(lgidx[:, t, :], lgmax[:, t, :], lg[:, t, :])
                own(ins)
                own(dve.tensor_copy(chosen[:, :], lgidx[:, :, 0]))
                dve.tensor_tensor(onehot[:, :, :], iota[:, 0:EXPERTS].unsqueeze(1).to_broadcast([TT, NT, EXPERTS]),
                                  chosen[:, :].unsqueeze(2).to_broadcast([TT, NT, EXPERTS]),
                                  ALU.is_equal).then_inc(onehot_ready, 1)
                if not last:
                    for f in range(2):
                        take_v(2, f, product(("v", 2, f), b))
                slot = product(("rk",), b)
                complete(dve, slot)
                rk = acc(slot[0])
                own(dve.tensor_tensor(place[:, :, :], rk[0:TT, 0:NT * EXPERTS].rearrange("p (t e) -> p t e", t=NT),
                                      filled[:, :].unsqueeze(1).to_broadcast([TT, NT, EXPERTS]), ALU.add))
                dve.tensor_tensor(filled[:, :], rk[0:TT, NT * EXPERTS:(NT + 1) * EXPERTS], filled[:, :],
                                  ALU.add).then_inc(free[slot[0]], 1)
                own(dve.tensor_tensor(place[:, :, :], place[:, :, :], onehot[:, :, :], ALU.mult))
                own(dve.tensor_reduce(place_f[:, :], place[:, :, :], AX.X, ALU.add))
                dve.wait_ge(lists_sent, 16 * NT * (b + 1))
                dve.tensor_copy(tok_id[:, :], tok_f[:, :])
                dve.tensor_copy(place_i[:, :], place_f[:, :]).then_inc(place_ready, 1)
                own(dve.tensor_scalar(tok_f[:, :], tok_f[:, :], float(BT), None, ALU.add))
                if not last:
                    assert steps[0] == OWN_PER_BLOCK, steps[0]

            with dve.Fori(0, NB - 1) as b:
                body(b, False)
            body(NB - 1, True)

            e8 = iota[0:1, 0:EXPERTS]
            j16 = iota[0:1, 0:FFT].unsqueeze(2).to_broadcast([1, FFT, EXPERTS])

            def over_tiles(row):
                return row.unsqueeze(1).to_broadcast([1, FFT, EXPERTS])

            own(dve.scalar_tensor_tensor(cnt[:, :], e8, -float(TOKENS), filled[0:1, :], ALU.mult, ALU.add))
            own(dve.tensor_scalar(tr[:, 0:9], iota[0:1, 0:9], float(SLOT), None, ALU.mult))
            own(dve.tensor_tensor(steps9[:, :, :], cnt[:, :].unsqueeze(2).to_broadcast([1, EXPERTS, 9]),
                                  tr[:, 0:9].unsqueeze(1).to_broadcast([1, EXPERTS, 9]), ALU.is_gt))
            own(dve.tensor_reduce(ntile[:, :], steps9[:, :, :], AX.X, ALU.add))
            own(dve.tensor_tensor_scan(tend[:, :], ones[0:1, 0:EXPERTS], ntile[:, :], 0.0, ALU.mult, ALU.add))
            own(dve.tensor_tensor(off[:, :], tend[:, :], ntile[:, :], ALU.subtract))
            own(dve.tensor_scalar(off[:, :], off[:, :], -float(SLOT), None, ALU.mult))
            own(dve.scalar_tensor_tensor(off[:, :], e8, float(TOKENS), off[:, :], ALU.mult, ALU.add))
            own(dve.tensor_tensor(grid[:, :, :], over_tiles(tend[:, :]), j16, ALU.is_le))
            own(dve.tensor_reduce(te[:, :], grid[:, :, :], AX.X, ALU.add))
            own(dve.tensor_tensor(grid[:, :, :], over_tiles(e8), te[:, :].unsqueeze(2).to_broadcast([1, FFT, EXPERTS]),
                                  ALU.is_equal))
            own(dve.scalar_tensor_tensor(grid2[:, :, :], j16, float(SLOT), over_tiles(off[:, :]), ALU.mult, ALU.add))
            own(dve.tensor_tensor(grid2[:, :, :], grid2[:, :, :], grid[:, :, :], ALU.mult))
            own(dve.tensor_reduce(tr[:, :], grid2[:, :, :], AX.X, ALU.add))
            own(dve.tensor_scalar(tr2[:, :], te[:, :], float(EXPERTS), float(LISTS), ALU.is_ge, ALU.mult))
            own(dve.tensor_tensor(tr[:, :], tr[:, :], tr2[:, :], ALU.add))
            own(dve.tensor_scalar(te7[:, :], te[:, :], float(EXPERTS - 1), None, ALU.min))
            dve.tensor_copy(tile_row[:, :], tr[:, :])
            dve.memset(xnB_lo.bitcast(F32), 0.0)
            dve.tensor_copy(tile_expert[:, :], te7[:, :]).then_inc(tiles_ready, 1)
            dve.wait_ge(tiles_ready, 1)

            def take_x(r, i):
                j = r * 4 + i
                e = dve.value_load(tile_expert[0:1, bass.ds(j, 1)], min_val=0, max_val=EXPERTS - 1)
                dve.wait_ge(fx_hi_ready, j + 1)
                dve.tensor_tensor(fxA_lo[i % 2], psum[0:DA, 7, 0:SLOT], fxA_hi[i % 2], ALU.subtract)
                dve.tensor_tensor(fxB_lo[i % 2][DB:2 * DB, :], psum[0:DB, 7, SLOT:2 * SLOT], fxB[i % 2][0:DB, :],
                                  ALU.subtract).then_inc(fx_ready, 1)
                dve.tensor_tensor(res[i % 4], xg[i % 4][:, 0:D], b2s[:, bass.ds(e, 1), :].rearrange("p o d -> p (o d)"),
                                  ALU.add).then_inc(res_ready, 1)

            def add_b1(r, i):
                j = r * 4 + i
                e = dve.value_load(tile_expert[0:1, bass.ds(j, 1)], min_val=0, max_val=EXPERTS - 1)
                for k, (lo, hi) in enumerate(((0, 512), (512, FF))):
                    dve.wait_ge(up_full, 2 * j + k + 1)
                    dve.tensor_tensor(hid[i % 2][:, lo:hi], psum[:, 2 * (i % 2) + k, 0:hi - lo],
                                      b1s[:, bass.ds(e, 1), lo:hi].rearrange("p o f -> p (o f)"),
                                      ALU.add).then_inc(biased, 1)

            def take_hidden(r, i):
                j = r * 4 + i
                dve.wait_ge(hidt_full, j + 1)
                dve.tensor_copy(hidT[i % 2][:, 0:512], psum[:, 4, :])
                dve.tensor_copy(hidT[i % 2][:, 512:FF], psum[:, 5, 0:FF - 512]).then_inc(hidt_ready, 1)

            def finish(r, i):
                j = r * 4 + i
                dve.wait_ge(down_full, j + 1)
                dve.wait_ge(res_ready, j + 1)
                dve.wait_ge(yo_free, j + 1)
                dve.tensor_tensor(yo[i % 4], psum[:, 6, 0:D], res[i % 4], ALU.add).then_inc(y_ready, 1)

            dve.wait_ge(b2_here, 16)
            take_x(0, 0)
            take_x(0, 1)
            dve.wait_ge(b1_here, 32)
            add_b1(0, 0)
            take_x(0, 2)
            add_b1(0, 1)

            def four_tiles(r, last):
                for i in range(4):
                    take_hidden(r, i)
                    if not last or i < 2:
                        add_b1(r, i + 2)
                    if not last or i < 1:
                        take_x(r, i + 3)
                    finish(r, i)

            with dve.Fori(0, FFT // 4 - 1) as r:
                four_tiles(r, False)
            four_tiles(FFT // 4 - 1, True)

        @block.gpsimd
        def _(pool):
            pools = [0]

            def own(ins):
                ins.then_inc(pool_step, 1)
                pools[0] += 1
                pool.wait_ge(pool_step, pools[0])

            pool.sem_inc(yo_free, 4)
            pool.sem_inc(w1_split, 1)
            pool.memset(ones[:, :], 1.0)
            own(pool.memset(ident[:, :], 0.0))
            pool.affine_select(out=ident[:, :], in_=ident[:, :], compare_op=ALU.not_equal, fill=1.0, base=0,
                               pattern=[[-1, P]], channel_multiplier=1).then_inc(ident_ready, 1)
            pool.memset(mask[:, :], 0.0)
            pool.memset(before[:, :], 1.0)
            pool.memset(all1[:, :], 1.0)
            pool.memset(minus_half[:, :], -0.5)
            pool.memset(zeros[:, :], 0.0)
            pool.memset(spare[:, :], SPARE_ROW)
            pool.iota(iota_i[:, :], pattern=[[1, 16]], base=0, channel_multiplier=0)
            pool.iota(place_i[:, :], pattern=[[TT, NT]], base=LISTS, channel_multiplier=1)
            pool.memset(tok_id[:, :], SPARE_ROW).then_inc(place_ready, 1)
            own(pool.iota(tok_i[:, :], pattern=[[TT, NT]], base=0, channel_multiplier=1))
            for r in range(1, REPR):
                pool.wait_ge(scaled, r + 1)
                own(pool.tensor_tensor(weff[:, CHANNELS - 1, :, :], wp_last[:, 0, :, :] if r == 1 else
                                       weff[:, CHANNELS - 1, :, :], wp_last[:, r, :, :], ALU.add))
            pool.engine_nop().then_inc(weff_ready, 1)
            pool.affine_select(out=before[:, :], in_=before[:, :], compare_op=ALU.is_gt, fill=0.0, base=0,
                               pattern=[[1, TT]], channel_multiplier=-1)
            images = GMAX // PER_IMAGE
            m3 = mask[:, :].rearrange("p (j n) -> p j n", n=PER_IMAGE)
            own(pool.affine_select(out=m3, in_=m3, compare_op=ALU.is_ge, fill=MASKED, base=0,
                                   pattern=[[-PER_IMAGE, images], [0, PER_IMAGE]], channel_multiplier=1))
            pool.affine_select(out=m3, in_=m3, compare_op=ALU.is_ge, fill=MASKED, base=PER_IMAGE - 1,
                               pattern=[[PER_IMAGE, images], [0, PER_IMAGE]],
                               channel_multiplier=-1).then_inc(consts_ready, 1)

            def inverse_std(kind, t, n_before, n_own):
                pool.wait_ge(ln_stats, n_before + 1)
                passed("pool", pool)
                pool.tensor_scalar(veps[:, kind, t:t + 1], mv[:, kind, t, 1:2], EPS, None,
                                   ALU.add).then_inc(pool_step, 1)
                pool.wait_ge(pool_step, n_own)
                pool.tensor_tensor(rstd[:, kind, t:t + 1], veps[:, kind, t:t + 1], minus_half[:, :],
                                   ALU.pow).then_inc(ln_rstd, 1)

            consts = pools[0]
            for t in range(NT):
                inverse_std(0, t, t, consts + t + 1)

            def send_places(n):
                pool.wait_ge(place_ready, n + 1)
                passed("pool", pool)
                for t in range(NT):
                    pool.indirect_dma_start(out=perm, out_offset=bass.IndirectOffsetOnAxis(ap=place_i[:, t:t + 1], axis=0),
                                            in_=tok_id[:, t:t + 1], in_offset=None).then_inc(lists_sent, 16)

            pool.wait_ge(inits_out, 32)
            def body(b, last):
                lns = NT + b * 2 * NT
                for s in range(NU + 1):
                    if s == 2:
                        pool.wait_ge(xn_ready, NT * b + NT)
                        pool.wait_ge(rows_ready, NT * b + 1)
                        passed("pool", pool)
                        pool.tensor_copy(hres[:, :, :], h[:, :, :]).then_inc(hres_ready, 1)
                    if s == 3:
                        send_places(b)
                    if 6 <= s < 9 and not last:
                        inverse_std(0, s - 6, lns + s - 6, consts + lns + s - 6 + 1)
                after = lns + (0 if last else NT)
                for t in range(NT):
                    inverse_std(1, t, after + t, consts + after + t + 1)
                if not last:
                    split_w1(b)

            def split_w1(b):
                cols = bass.ds(b * W1_PIECE, W1_PIECE)
                pool.wait_ge(w1_hi_ready, b + 1)
                pool.tensor_tensor(w1A_lo[:, cols], w1A_in[:, cols], w1A_hi[:, cols],
                                   ALU.subtract).then_inc(w1A_split, 1)
                pool.wait_ge(w1A_split, b + 1)
                pool.tensor_tensor(w1B[0:DB, cols], w1B_in[0:DB, cols], w1B_part[:, :],
                                   ALU.subtract).then_inc(w1_split, 1)

            with pool.Fori(0, NB - 1) as b:
                body(b, False)
            body(NB - 1, True)
            send_places(NB)

            def gather(j):
                pool.wait_ge(ids_here[j], 16)
                if j >= 4:
                    pool.wait_ge(res_ready, j - 3)
                pool.indirect_dma_start(out=xg[j % 4], out_offset=None, in_=table,
                                        in_offset=bass.IndirectOffsetOnAxis(ap=ids[:, j:j + 1], axis=0)
                                        ).then_inc(xg_here[j % 4], 16)

            for j in range(4):
                gather(j)
            for j in range(FFT):
                if j + 4 < FFT:
                    gather(j + 4)
                pool.wait_ge(y_ready, j + 2)
                pool.indirect_dma_start(out=out, out_offset=bass.IndirectOffsetOnAxis(ap=ids[:, j:j + 1], axis=0),
                                        in_=yo[j % 4], in_offset=None, bounds_check=TOKENS - 1,
                                        oob_is_err=False).then_inc(out_sent[j % 4], 16)
                if j >= 2:
                    pool.wait_ge(out_sent[(j - 2) % 4], 16 * ((j - 2) // 4 + 1))
                    pool.sem_inc(yo_free, 1)
            for j in (FFT - 2, FFT - 1):
                pool.wait_ge(out_sent[j % 4], 16 * (j // 4 + 1))


OWN_PER_BLOCK = 2 * NU + 2 * NT + 2 + 1 + 1 + 3


def kernel(x, L0_tok_W_repr, L0_tok_b_repr, L0_tok_W_proj, L0_tok_b_proj, L0_attn_W_qkv, L0_attn_W_out,
           L0_ffn_gate_w, L0_ffn_gate_b, L0_ffn_w1, L0_ffn_b1, L0_ffn_w2, L0_ffn_b2):
    from concourse import bacc
    from concourse.bass_utils import run_bass_kernel_spmd

    half = PATCH // 2
    per = IMAGES // NB
    arrays = {
        "xT": np.asarray(x).reshape(NB, per, CHANNELS, GRID, 2, half, GRID, PATCH)
        .transpose(0, 5, 7, 2, 4, 1, 3, 6).reshape(NB, P, KX, BT),
        "w_proj": np.asarray(L0_tok_W_proj).reshape(REPR, D, 2, P).transpose(3, 2, 0, 1),
        "w_repr": np.asarray(L0_tok_W_repr).reshape(REPR * CHANNELS),
        "b_repr": np.asarray(L0_tok_b_repr),
        "b_proj": np.asarray(L0_tok_b_proj),
        "w_qkv": np.asarray(L0_attn_W_qkv).T,
        "w_out": np.asarray(L0_attn_W_out).T.reshape(PAIRS, P, D).transpose(1, 0, 2),
        "gate_w": np.asarray(L0_ffn_gate_w),
        "gate_b": np.asarray(L0_ffn_gate_b).reshape(1, EXPERTS),
        "w1": np.asarray(L0_ffn_w1).transpose(1, 0, 2).reshape(D, EXPERTS * FF),
        "b1": np.asarray(L0_ffn_b1),
        "w2": np.asarray(L0_ffn_w2).reshape(EXPERTS, FCH, P, D).transpose(2, 0, 1, 3),
        "b2": np.asarray(L0_ffn_b2),
    }
    nc = bacc.Bacc("TRN2", target_bir_lowering=False, num_devices=1)
    args = []
    for name in arrays:
        arrays[name] = np.ascontiguousarray(arrays[name])
        args.append(nc.dram_tensor(name, arrays[name].shape, F32, kind="ExternalInput").ap())
    args.append(nc.dram_tensor("out", [TOKENS, D], F32, kind="ExternalOutput").ap())
    build(nc, *args)
    r = run_bass_kernel_spmd(nc, [arrays], core_ids=[0])
    return r.results[0]["out"].reshape(IMAGES, PER_IMAGE, D)
```

```python
from contextlib import ExitStack

import numpy as np

import concourse.bass as bass
from concourse import mybir

ALU = mybir.AluOpType
ACT = mybir.ActivationFunctionType
AX = mybir.AxisListType
F32 = mybir.dt.float32
F32R = mybir.dt.float32r
BF16 = mybir.dt.bfloat16
U32 = mybir.dt.uint32
I32 = mybir.dt.int32

IMAGES, CHANNELS, SIDE, PATCH = 32, 3, 96, 16
GRID = SIDE // PATCH
PER_IMAGE = GRID * GRID
TOKENS = IMAGES * PER_IMAGE
REPR, D = 5, 192
HEADS, DH = 12, 64
HD = HEADS * DH
EXPERTS, FF = 8, 768
P = 128

NB = 4
BT = TOKENS // NB
TT = 96
NT = BT // TT
KX = CHANNELS * PATCH * PATCH // P
DA, DB = 128, 64
PAIRS = HEADS // 2
GROUPS = [(0, 108), (108, 108), (216, 72)]
GMAX = 108
HQ = 4
UNITS = [(q, g) for q in range(HEADS // HQ) for g in range(len(GROUPS))]
NU = len(UNITS)
AHEAD = 2
LAG_T, LAG_AV = 1, 2
EPS = 1e-5
LOGIT_SCALE = 8.0
MASKED = -1.0e30

SLOT = 128
FFT = (TOKENS + EXPERTS * (SLOT - 1)) // SLOT
FCH = FF // P
SPARE_ROW = TOKENS
LISTS = EXPERTS * TOKENS
SPARE_SLOTS = 3 * P
PERM_COLS = (LISTS + SPARE_SLOTS) // P

W1_PIECE = EXPERTS * FF // (NB - 1)

WQ_PIECES = [slice(0, HD + HQ * DH), slice(HD + HQ * DH, 3 * HD)]

ACC = [0, 1, 2, 3]
SC_BANK, TR_BANK, AV_BANK = 4, 5, 6


def per_block_products(last):
    order = []
    for s in range(NU + LAG_AV):
        order += step_products(s, last)
    if not last:
        order += [("q", 0), ("k", 0), ("q", 1), ("k", 1)]
        order += [("gt", 0), ("v", 0, 0), ("gt", 1), ("v", 0, 1), ("gt", 2), ("v", 1, 0),
                  ("lg",), ("v", 1, 1), ("v", 2, 0), ("v", 2, 1), ("rk",)]
    else:
        order += [("gt", 0), ("gt", 1), ("gt", 2), ("lg",), ("rk",)]
    return order


def step_products(s, last):
    if s < 5:
        qk = [[("q", 2), ("k", 2), ("q", 3)], [("k", 3)], [("q", 4)], [("k", 4), ("q", 5)], [("k", 5)]][s]
        return qk + ([("tok", 0)] if s == 4 and not last else [])
    if last:
        return [[("o", 0)], [("o", 1)], [("o", 2)]][s - 8] if s >= 8 else []
    return [[("tok", 1)], [("tok", 2)], [("xt", 0)], [("xt", 1)], [("xt", 2), ("o", 0)], [("o", 1), ("o", 2)]][s - 5]


OPENING = ([("tok", 0), ("bias",), ("tok", 1), ("tok", 2)] + [("xt", t) for t in range(NT)]
           + [("q", 0), ("k", 0), ("q", 1), ("k", 1)] + [("v", g, f) for g in range(3) for f in range(2)])
MIDDLE, FINAL = per_block_products(False), per_block_products(True)
assert len(MIDDLE) % len(ACC) == 0


def product(key, b, opening=False):
    if opening:
        n, blocks = OPENING.index(key), 0
    elif isinstance(b, int) and b == NB - 1:
        n, blocks = len(OPENING) + FINAL.index(key), b
    else:
        n, blocks = len(OPENING) + MIDDLE.index(key), b
    return n % len(ACC), n // len(ACC) + blocks * (len(MIDDLE) // len(ACC))


def build(nc, xT, w_proj, w_repr, b_repr, b_proj, w_qkv, w_out, gate_w, gate_b, w1, b1, w2, b2, out):
    table = nc.dram_tensor("token_table", [TOKENS + 1, 2 * D], F32, kind="Internal").ap()
    perm = nc.dram_tensor("expert_lists", [LISTS + SPARE_SLOTS, 1], U32, kind="Internal").ap()

    with ExitStack() as ctx:
        def sb(name, shape, dt=F32):
            return ctx.enter_context(nc.sbuf_tensor(name, shape, dt))

        def sb_shared(*tensors):
            handles = []
            for i, (name, shape, dt) in enumerate(tensors):
                if i < len(tensors) - 1:
                    with nc.sbuf_tensor(name, shape, dt) as t:
                        handles.append(t)
                else:
                    handles.append(sb(name, shape, dt))
            return handles

        def sem(name):
            return ctx.enter_context(nc.semaphore(name))

        psum = ctx.enter_context(nc.psum_tensor("psum", [P, 8, 512], F32))

        wr = sb("wr", [P, REPR * CHANNELS])
        br = sb("br", [P, REPR])
        bp = sb("bp", [REPR, D])
        late = sb("late", [P, EXPERTS * FF])
        b1s = late[:, :].rearrange("p (e f) -> p e f", e=EXPERTS)
        v_cols, p_cols = len(GROUPS) * HD, 3 * HQ * GMAX
        v = late[:, 0:v_cols].rearrange("p (g c) -> p g c", g=len(GROUPS))
        probs = late[0:GMAX, v_cols:v_cols + p_cols].rearrange("p (s n) -> p s n", s=3)
        probsT = late[0:GMAX, v_cols + p_cols:v_cols + 2 * p_cols].rearrange("p (s n) -> p s n", s=3)
        w_first = v_cols + 2 * p_cols
        weff = late[:, w_first:w_first + 2 * CHANNELS * D].rearrange("p (c h e) -> p c h e", c=CHANNELS, h=2)
        wb = sb("wb", [P, 2, D])
        bias = sb("bias", [TT, D])
        w2s, wq_in, wq_parts = sb_shared(("w2s", [P, EXPERTS, FCH, D], F32), ("wq_in", [P, 4, 3 * HD], F32),
                                         ("wq_parts", [P, 4, 3 * HD], F32R))
        wqA_hi, wqA_lo, wqB = [wq_parts[:, i, :] for i in range(3)]
        wqA_in, wqB_in = wq_in[:, 1, :], wq_in[:, 3, :]
        wo = sb("wo", [P, PAIRS, D])
        gwA = sb("gwA", [DA, EXPERTS])
        gwB = sb("gwB", [DB + 1, EXPERTS])
        w1A_hi = sb("w1A_hi", [DA, EXPERTS * FF], F32R)
        w1A_in, w1A_lo = sb_shared(("w1A_in", [DA, EXPERTS * FF], F32), ("w1A_lo", [DA, EXPERTS * FF], F32R))
        wp_last = w1A_in[:, 0:2 * REPR * D].rearrange("p (r h e) -> p r h e", r=REPR, h=2)
        w1B_in, w1B = sb_shared(("w1B_in", [2 * DB, EXPERTS * FF], F32), ("w1B", [2 * DB, EXPERTS * FF], F32R))
        w1B_part = sb("w1B_part", [DB, W1_PIECE], F32R)
        ident = sb("ident", [P, P])
        ones = sb("ones", [P, TT])
        mask = sb("mask", [GMAX, GMAX])
        before = sb("before", [TT, TT], BF16)
        all1 = sb("all1", [TT, TT], BF16)
        minus_half = sb("minus_half", [TT, 1])
        iota_i = sb("iota_i", [TT, 16], I32)
        iota = sb("iota", [TT, 16])
        tok_i = sb("tok_i", [TT, NT], I32)
        tok_f = sb("tok_f", [TT, NT])
        xb = sb("xb", [P, KX, BT])
        h = sb("h", [TT, NT, D])
        hres = sb("hres", [TT, NT, D])
        xn_hi = sb("xn_hi", [P, 2, BT], F32R)
        xnA_lo = sb("xnA_lo", [DA, BT], F32R)
        xnB_lo2 = sb("xnB_lo2", [2 * DB, BT], F32R)
        xnB_lo = xnB_lo2[0:DB, :]
        xnA_hi, xnB = xn_hi[:, 0, :], xn_hi[:, 1, :]
        qT = sb("qT", [P, PAIRS, BT])
        kT = sb("kT", [P, PAIRS, 2, BT])
        wp = late[:, 0:2 * REPR * D].rearrange("p (h r e) -> p h r e", h=2, r=REPR)
        oT = sb("oT", [P, PAIRS, BT])
        top = sb("top", [GMAX, 3, HQ])
        total = sb("total", [GMAX, 3, HQ])
        share = sb("share", [GMAX, 3, HQ])
        rows = sb("rows", [TT, NT, 2 * D])
        xn = rows[:, :, D:2 * D]
        xn2A = sb("xn2A", [DA, BT])
        xn2B = sb("xn2B", [DB + 1, BT])
        stats = sb("stats", [TT, 2, NT, 6])
        mv = sb("mv", [TT, 2, NT, 2])
        veps = sb("veps", [TT, 2, NT])
        rstd = sb("rstd", [TT, 2, NT])
        lg = sb("lg", [TT, NT, EXPERTS])
        lgmax = sb("lgmax", [TT, NT, 8])
        lgidx = sb("lgidx", [TT, NT, 8], U32)
        chosen = sb("chosen", [TT, NT])
        onehot = sb("onehot", [TT, NT, EXPERTS], BF16)
        place = sb("place", [TT, NT, EXPERTS])
        place_f = sb("place_f", [TT, NT])
        place_i = sb("place_i", [TT, NT], U32)
        tok_id = sb("tok_id", [TT, NT], U32)
        filled = sb("filled", [TT, EXPERTS])
        steps9 = sb("steps9", [1, EXPERTS, 9])
        cnt = sb("cnt", [1, EXPERTS])
        ntile = sb("ntile", [1, EXPERTS])
        tend = sb("tend", [1, EXPERTS])
        off = sb("off", [1, EXPERTS])
        grid = sb("grid", [1, FFT, EXPERTS])
        grid2 = sb("grid2", [1, FFT, EXPERTS])
        te = sb("te", [1, FFT])
        te7 = sb("te7", [1, FFT])
        tr = sb("tr", [1, FFT])
        tr2 = sb("tr2", [1, FFT])
        tile_expert = sb("tile_expert", [1, FFT], I32)
        tile_row = sb("tile_row", [1, FFT], I32)
        ids = sb("ids", [SLOT, FFT], U32)
        zeros = sb("zeros", [1, 2 * D])
        spare = sb("spare", [P, PERM_COLS], U32)
        xbf = xb[:, :, :].rearrange("p k n -> p (k n)")
        xg = [xbf[:, i * 2 * D:(i + 1) * 2 * D] for i in range(4)]
        fxA_hi, fxA_lo, fxB, fxB_lo = [[w[:, i * SLOT:(i + 1) * SLOT] for i in range(2)]
                                       for w in (xnA_hi, xnA_lo, xnB, xnB_lo2[:, :])]
        qTf = qT[:, :, :].rearrange("p k n -> p (k n)")
        kTf = kT[:, :, :, :].rearrange("p k i n -> p (k i n)")
        oTf = oT[:, :, :].rearrange("p k n -> p (k n)")
        hid = [qTf[:, 0:FF], qTf[:, FF:2 * FF]]
        hidT = [kTf[:, 0:FF], kTf[:, FF:2 * FF]]
        b2s = kTf[:, 2 * FF:2 * FF + EXPERTS * D].rearrange("p (e d) -> p e d", e=EXPERTS)
        res = [oTf[:, i * D:(i + 1) * D] for i in range(4)]
        yo = [oTf[:, (4 + i) * D:(5 + i) * D] for i in range(4)]

        x_here = sem("x_here")
        wp_here = sem("wp_here")
        br_here = sem("br_here")
        wq_here = [sem(f"wq_here{i}") for i in range(len(WQ_PIECES))]
        wq_hi_ready = sem("wq_hi_ready")
        w1_here = sem("w1_here")
        w1_hi_ready = sem("w1_hi_ready")
        w1A_split, w1_split = sem("w1A_split"), sem("w1_split")
        wq_split = sem("wq_split")
        wo_here = sem("wo_here")
        w2_here = sem("w2_here")
        b1_here = sem("b1_here")
        b2_here = sem("b2_here")
        inits_out = sem("inits_out")
        full = [sem(f"acc_full{i}") for i in ACC]
        free = [sem(f"acc_free{i}") for i in ACC]
        sc_full, sc_free = sem("sc_full"), sem("sc_free")
        tr_full, tr_free = sem("tr_full"), sem("tr_free")
        av_full, av_free = sem("av_full"), sem("av_free")
        top_ready = sem("top_ready")
        exp_ready = sem("exp_ready")
        probs_ready = sem("probs_ready")
        ln_stats = sem("ln_stats")
        ln_rstd = sem("ln_rstd")
        xn_ready = sem("xn_ready")
        xn_hi_ready = sem("xn_hi_ready")
        rows_ready = sem("rows_ready")
        hres_ready = sem("hres_ready")
        onehot_ready = sem("onehot_ready")
        place_ready = sem("place_ready")
        rows_sent = sem("rows_sent")
        lists_sent = sem("lists_sent")
        dve_step = sem("dve_step")
        pool_step = sem("pool_step")
        waited = {"dve": sem("dve_waited"), "pool": sem("pool_waited")}
        ident_ready = sem("ident_ready")
        consts_ready = sem("consts_ready")
        weff_ready = sem("weff_ready")
        scaled = sem("scaled")
        wb_ready = sem("wb_ready")
        kt_zero = sem("kt_zero")
        tiles_ready = sem("tiles_ready")
        ids_here = [sem(f"ids_here{j}") for j in range(FFT)]
        xg_here = [sem(f"xg_here{i}") for i in range(4)]
        fxt_full, fx_hi_ready, fx_ready = sem("fxt_full"), sem("fx_hi_ready"), sem("fx_ready")
        up_full, biased, hid_ready = sem("up_full"), sem("biased"), sem("hid_ready")
        hidt_full, hidt_ready, hidt_rest_ready = sem("hidt_full"), sem("hidt_ready"), sem("hidt_rest_ready")
        down_full, y_ready = sem("down_full"), sem("y_ready")
        res_ready = sem("res_ready")
        yo_free = sem("yo_free")
        out_sent = [sem(f"out_sent{i}") for i in range(4)]

        def acc(bank):
            return psum[:, ACC[bank], :]

        def taken(eng, slot):
            bank, before_it = slot
            eng.wait_ge(free[bank], before_it + 1)

        def all_taken(eng, keys, b, opening=False, following=None):
            last = {}
            for key in keys:
                last[product(key, b, opening)[0]] = product(key, b, opening)
            for bank, slot in last.items():
                if following is None or bank != following[0]:
                    taken(eng, slot)

        def complete(eng, slot):
            bank, before_it = slot
            eng.wait_ge(full[bank], before_it + 1)

        def passed(name, eng):
            eng.sem_inc(waited[name], 1)

        def unit(u):
            q, g = UNITS[u]
            return (q, g) + GROUPS[g]

        block = ctx.enter_context(nc.Block())

        @block.sync
        def _(sp):
            sp.sem_inc(rows_sent, 16)
            sp.dma_start(wr[:, :], w_repr.partition_broadcast(P)).then_inc(wp_here, 16)
            sp.dma_start(wp, w_proj).then_inc(wp_here, 16)
            sp.dma_start(xb[:, :, :], xT[0]).then_inc(x_here, 16)
            sp.dma_start(br[:, :], b_repr.partition_broadcast(P)).then_inc(br_here, 16)
            sp.dma_start(bp[:, :], b_proj).then_inc(br_here, 16)
            for i, cols in enumerate(WQ_PIECES):
                sp.dma_start(wqA_in[:, cols], w_qkv[0:DA, cols]).then_inc(wq_here[i], 16)
                sp.dma_start(wqB_in[0:DB, cols], w_qkv[DA:D, cols]).then_inc(wq_here[i], 16)
            sp.dma_start(wo[:, :, :], w_out).then_inc(wo_here, 16)
            sp.dma_start(gwA[:, :], gate_w[0:DA, :]).then_inc(wo_here, 16)
            sp.dma_start(gwB[0:DB, :], gate_w[DA:D, :]).then_inc(wo_here, 16)
            sp.dma_start(gwB[DB:DB + 1, :], gate_b).then_inc(wo_here, 16)
            sp.wait_ge(consts_ready, 1)
            sp.dma_start(perm.rearrange("(p c) o -> p (c o)", c=PERM_COLS), spare[:, :]).then_inc(inits_out, 16)
            sp.dma_start(table[SPARE_ROW:SPARE_ROW + 1, :], zeros[:, :]).then_inc(inits_out, 16)

            def body(b, last):
                if not last:
                    sp.wait_ge(xn_ready, NT * b + NT)
                    sp.dma_start(xb[:, :, :], xT[b + 1]).then_inc(x_here, 16)
                sp.wait_ge(rows_ready, NT * b + NT + 1)
                sp.dma_start(table[bass.ds(b * BT, BT), :].rearrange("(t p) d -> p t d", p=TT),
                             rows[:, :, :]).then_inc(rows_sent, 16)

            with sp.Fori(0, NB - 1) as b:
                body(b, False)
            complete(sp, product(("k", PAIRS - 1), NB - 1))
            sp.dma_start(w2s[:, :, :, :], w2).then_inc(w2_here, 16)
            sp.wait_ge(sc_full, NU * NB)
            sp.dma_start(b2s, b2.partition_broadcast(P)).then_inc(b2_here, 16)
            sp.wait_ge(av_full, NU * NB)
            sp.dma_start(b1s[:, 0:EXPERTS // 2, :], b1[0:EXPERTS // 2].partition_broadcast(P)).then_inc(b1_here, 16)
            body(NB - 1, True)
            sp.dma_start(b1s[:, EXPERTS // 2:, :], b1[EXPERTS // 2:].partition_broadcast(P)).then_inc(b1_here, 16)

            sp.wait_ge(rows_sent, 16 * NB + 16)
            sp.wait_ge(lists_sent, 16 * NT * (NB + 1))
            sp.wait_ge(tiles_ready, 1)
            for j in range(FFT):
                row = sp.value_load(tile_row[0:1, j:j + 1], min_val=0, max_val=LISTS)
                sp.dma_start(ids[:, j:j + 1], perm[bass.ds(row, SLOT), :]).then_inc(ids_here[j], 16)

        @block.tensor
        def _(pe):
            def into(slot):
                bank, before_it = slot
                pe.wait_ge(free[bank], before_it)
                return acc(bank)

            def tokens(t, slot):
                dst = into(slot)
                for k in range(KX):
                    mm = pe.matmul(dst[0:TT, 0:D], xb[:, k, t * TT:(t + 1) * TT], weff[:, k // 2, k % 2, :],
                                   start=(k == 0), stop=(k == KX - 1))
                mm.then_inc(full[slot[0]], 1)

            def turn_xn(t, slot, ready, src, col):
                dst = into(slot)
                pe.wait_ge(*ready)
                pe.transpose(dst[0:DA, 0:TT], src[:, t, col:col + DA], ident[0:TT, 0:TT])
                pe.transpose(dst[0:DB, TT:2 * TT], src[:, t, col + DA:col + D],
                             ident[0:TT, 0:TT]).then_inc(full[slot[0]], 1)

            def split_product(dst, parts):
                for i, (lhsT, rhs) in enumerate(parts):
                    mm = pe.matmul(dst, lhsT, rhs, start=(i == 0), stop=(i == len(parts) - 1))
                return mm

            def heads(which, c, slot):
                dst = into(slot)
                col = (0 if which == "q" else HD) + c * P
                cs = slice(col, col + P)
                split_product(dst[:, 0:BT], [
                    (wqA_hi[:, cs], xnA_hi), (wqA_hi[:, cs], xnA_lo[:, :]), (wqA_lo[:, cs], xnA_hi),
                    (wqB[:, cs], xnB), (wqB[0:DB, cs], xnB_lo)]).then_inc(full[slot[0]], 1)

            def values(g, f, slot):
                dst = into(slot)
                t0, n = GROUPS[g]
                col = 2 * HD + f * (HD // 2)
                ts, cs = slice(t0, t0 + n), slice(col, col + HD // 2)
                split_product(dst[0:n, 0:HD // 2], [
                    (xnA_hi[:, ts], wqA_hi[:, cs]), (xnA_lo[:, ts], wqA_hi[:, cs]), (xnA_hi[:, ts], wqA_lo[:, cs]),
                    (xnB[:, ts], wqB[:, cs]), (xnB_lo[:, ts], wqB[0:DB, cs])]).then_inc(full[slot[0]], 1)

            def scores(u, b):
                q, g, t0, n = unit(u)
                pe.wait_ge(sc_free, NU * b + u + 1)
                for i in range(2):
                    c = 2 * q + i
                    dst = psum[0:n, SC_BANK, 2 * i * n:2 * (i + 1) * n].rearrange("p (i n) -> p i n", i=2)
                    mm = pe.matmul(dst, qT[:, c, t0:t0 + n], kT[:, c, :, t0:t0 + n], start=True, stop=True)
                mm.then_inc(sc_full, 1)

            def turn_probs(u, b):
                q, g, t0, n = unit(u)
                pe.wait_ge(probs_ready, NU * b + u + 1)
                pe.wait_ge(tr_free, NU * b + u + 1)
                for i in range(HQ):
                    mm = pe.transpose(psum[0:n, TR_BANK, i * n:(i + 1) * n], probs[0:n, u % 3, i * n:(i + 1) * n],
                                      ident[0:n, 0:n])
                mm.then_inc(tr_full, 1)

            def attend(u, b):
                q, g, t0, n = unit(u)
                pe.wait_ge(tr_free, NU * b + u + 2)
                pe.wait_ge(av_free, NU * b + u + 1)
                for i in range(2):
                    c = 2 * q + i
                    mm = pe.matmul(psum[:, AV_BANK, 2 * i * n:2 * (i + 1) * n], v[0:n, g, c * P:(c + 1) * P],
                                   probsT[0:n, u % 3, 2 * i * n:2 * (i + 1) * n], start=True, stop=True)
                mm.then_inc(av_full, 1)

            def project(t, slot, b, c0=0, c1=PAIRS):
                dst = into(slot) if c0 == 0 else acc(slot[0])
                pe.wait_ge(av_free, NU * b + NU * c1 // PAIRS + 1)
                for c in range(c0, c1):
                    mm = pe.matmul(dst[0:TT, 0:D], oT[:, c, t * TT:(t + 1) * TT], wo[:, c, :],
                                   start=(c == 0), stop=(c == PAIRS - 1))
                if c1 == PAIRS:
                    mm.then_inc(full[slot[0]], 1)

            def gate(b):
                slot = product(("lg",), b)
                all_taken(pe, [("gt", t) for t in range(NT)], b, following=slot)
                dst = into(slot)
                for t in range(NT):
                    pe.matmul(dst[0:TT, t * EXPERTS:(t + 1) * EXPERTS], xn2A[:, t * TT:(t + 1) * TT], gwA[:, :],
                              start=True, stop=False)
                    mm = pe.matmul(dst[0:TT, t * EXPERTS:(t + 1) * EXPERTS], xn2B[:, t * TT:(t + 1) * TT], gwB[:, :],
                                   start=False, stop=True)
                mm.then_inc(full[slot[0]], 1)

            def ranks(b):
                slot = product(("rk",), b)
                dst = into(slot)
                pe.wait_ge(onehot_ready, b + 1)
                for t in range(NT):
                    col = t * EXPERTS
                    for e in range(t):
                        pe.matmul(dst[0:TT, col:col + EXPERTS], all1[:, :], onehot[:, e, :],
                                  start=(e == 0), stop=False)
                    pe.matmul(dst[0:TT, col:col + EXPERTS], before[:, :], onehot[:, t, :], start=(t == 0), stop=True)
                col = NT * EXPERTS
                for t in range(NT):
                    mm = pe.matmul(dst[0:TT, col:col + EXPERTS], all1[:, :], onehot[:, t, :],
                                   start=(t == 0), stop=(t == NT - 1))
                mm.then_inc(full[slot[0]], 1)

            def keep_clock(n):
                for _ in range(n):
                    pe.transpose(psum[:, TR_BANK, 0:P], ident[:, :], ident[:, :])

            pe.wait_ge(ident_ready, 1)
            pe.wait_ge(wp_here, 32)
            keep_clock(32)
            pe.wait_ge(x_here, 16)
            pe.wait_ge(weff_ready, 2)
            tokens(0, product(("tok", 0), 0, opening=True))
            pe.wait_ge(br_here, 32)
            pe.wait_ge(wb_ready, 1)
            slot = product(("bias",), 0, opening=True)
            dst = into(slot)
            pe.matmul(dst[0:TT, 0:D], ones[:, :], wb[:, 0, :], start=True, stop=False)
            pe.matmul(dst[0:TT, 0:D], ones[:, :], wb[:, 1, :], start=False, stop=False)
            pe.matmul(dst[0:TT, 0:D], ones[0:REPR, :], bp[:, :], start=False, stop=True).then_inc(full[slot[0]], 1)
            for t in range(1, NT):
                tokens(t, product(("tok", t), 0, opening=True))
            for t in range(NT):
                turn_xn(t, product(("xt", t), 0, opening=True), (xn_ready, t + 1), xn, 0)
            pe.wait_ge(wq_hi_ready, 2)
            pe.wait_ge(wq_split, 2)
            all_taken(pe, [("xt", t) for t in range(NT)], 0, opening=True)
            for c in range(2):
                heads("q", c, product(("q", c), 0, opening=True))
                heads("k", c, product(("k", c), 0, opening=True))
            pe.wait_ge(wq_hi_ready, 4)
            pe.wait_ge(wq_split, 4)
            for g in range(3):
                for f in range(2):
                    values(g, f, product(("v", g, f), 0, opening=True))
                    if g == 0:
                        if f == 0:
                            all_taken(pe, [(w, c) for c in range(2) for w in "qk"], 0, opening=True)
                        scores(f, 0)

            def body(b, last):
                for s in range(NU + LAG_AV):
                    for key in step_products(s, last):
                        slot = product(key, b)
                        if key[0] == "tok":
                            if key[1] == 0:
                                pe.wait_ge(x_here, 16 * b + 32)
                            tokens(key[1], slot)
                        elif key[0] == "xt":
                            turn_xn(key[1], slot, (xn_ready, NT * b + NT + key[1] + 1), xn, 0)
                        elif key[0] == "o":
                            project(key[1], slot, b, 0, PAIRS - 2)
                        else:
                            heads(*key, slot)
                    if LAG_T <= s < NU + LAG_T:
                        turn_probs(s - LAG_T, b)
                    if s >= LAG_AV:
                        attend(s - LAG_AV, b)
                    if s + AHEAD < NU:
                        if (s + AHEAD) % 3 == 0:
                            c = 2 * ((s + AHEAD) // 3)
                            all_taken(pe, [(w, i) for i in (c, c + 1) for w in "qk"], b)
                        scores(s + AHEAD, b)
                if not last:
                    slot = product(("q", 0), b)
                    all_taken(pe, [("xt", t) for t in range(NT)], b, following=slot)
                    heads("q", 0, slot)
                for t in range(NT):
                    project(t, product(("o", t), b), b, PAIRS - 2)
                if not last:
                    for w, c in (("k", 0), ("q", 1), ("k", 1)):
                        heads(w, c, product((w, c), b))
                for t in range(NT):
                    turn_xn(t, product(("gt", t), b), (rows_ready, NT * b + t + 2), rows, D)
                    if not last:
                        for g, f in [[(0, 0)], [(0, 1)], [(1, 0)]][t]:
                            values(g, f, product(("v", g, f), b))
                        if t < AHEAD:
                            if t == 0:
                                all_taken(pe, [(w, c) for c in range(2) for w in "qk"], b)
                            scores(t, b + 1)
                gate(b)
                if not last:
                    for g, f in ((1, 1), (2, 0), (2, 1)):
                        values(g, f, product(("v", g, f), b))
                ranks(b)

            pe.wait_ge(wo_here, 64)
            with pe.Fori(0, NB - 1) as b:
                body(b, False)
            body(NB - 1, True)

            def turn_x(r, i):
                j = r * 4 + i
                pe.wait_ge(xg_here[i % 4], r * 16 + 16 * (i // 4 + 1))
                pe.wait_ge(fx_ready, j)
                pe.transpose(psum[0:DA, 7, 0:SLOT], xg[i % 4][:, D:D + DA], ident[:, :])
                pe.transpose(psum[0:DB, 7, SLOT:2 * SLOT], xg[i % 4][:, D + DA:2 * D],
                             ident[:, :]).then_inc(fxt_full, 1)

            def up(r, i):
                j = r * 4 + i
                e = pe.value_load(tile_expert[0:1, bass.ds(j, 1)], min_val=0, max_val=EXPERTS - 1)
                pe.wait_ge(fx_ready, j + 1)
                p2 = i % 2
                for lo, hi in ((0, 512), (512, FF)):
                    wA, wA_lo, wB = [w.rearrange("p (e f) -> p e f", e=EXPERTS)[:, bass.ds(e, 1), lo:hi]
                                     for w in (w1A_hi[:, :], w1A_lo[:, :], w1B[:, :])]
                    split_product(psum[:, 2 * p2 + lo // 512, 0:hi - lo], [
                        (fxA_hi[p2], wA), (fxA_lo[p2], wA), (fxA_hi[p2], wA_lo),
                        (fxB[p2], wB), (fxB_lo[p2], wB)]).then_inc(up_full, 1)

            def turn_hidden(r, i):
                j = r * 4 + i
                pe.wait_ge(hid_ready, j + 1)
                pe.wait_ge(hidt_ready, j + 1)
                pe.wait_ge(hidt_rest_ready, j + 1)
                for c in range(FCH):
                    mm = pe.transpose(psum[:, 4 + c // 4, (c % 4) * P:(c % 4 + 1) * P],
                                      hid[i % 2][:, c * P:(c + 1) * P], ident[:, :])
                    if c in (3, FCH - 1):
                        mm.then_inc(hidt_full, 1)

            def down(r, i):
                j = r * 4 + i
                e = pe.value_load(tile_expert[0:1, bass.ds(j, 1)], min_val=0, max_val=EXPERTS - 1)
                pe.wait_ge(hidt_ready, j + 2)
                pe.wait_ge(hidt_rest_ready, j + 2)
                pe.wait_ge(y_ready, j + 1)
                for c in range(FCH):
                    mm = pe.matmul(psum[:, 6, 0:D], hidT[i % 2][:, c * P:(c + 1) * P],
                                   w2s[:, bass.ds(e, 1), c, :], start=(c == 0), stop=(c == FCH - 1))
                mm.then_inc(down_full, 1)

            pe.wait_ge(tiles_ready, 1)
            pe.wait_ge(w1_split, NB)
            pe.wait_ge(w2_here, 16)
            pe.wait_ge(ids_here[0], 16)
            keep_clock(16)
            turn_x(0, 0)
            up(0, 0)
            turn_x(0, 1)
            up(0, 1)
            turn_x(0, 2)

            def four_tiles(r, last):
                for i in range(4):
                    turn_hidden(r, i)
                    if not last or i < 2:
                        up(r, i + 2)
                    if not last or i < 1:
                        turn_x(r, i + 3)
                    down(r, i)

            with pe.Fori(0, FFT // 4 - 1) as r:
                four_tiles(r, False)
            four_tiles(FFT // 4 - 1, True)

        @block.scalar
        def _(act):
            act.sem_inc(tr_free, 1)
            act.sem_inc(av_free, 1)
            act.sem_inc(hidt_rest_ready, 1)
            act.wait_ge(wp_here, 32)
            for r in range(REPR):
                s = (r + 1) * CHANNELS - 1
                act.activation(wp_last[:, r, :, :], wp[:, :, r, :], ACT.Identity,
                               scale=wr[:, s:s + 1]).then_inc(scaled, 1)
            for i, cols in enumerate(WQ_PIECES):
                act.wait_ge(wq_here[i], 32)
                act.copy(wqA_hi[:, cols], wqA_in[:, cols]).then_inc(wq_hi_ready, 1)
                act.copy(wqB[0:DB, cols], wqB_in[0:DB, cols]).then_inc(wq_hi_ready, 1)
            act.wait_ge(weff_ready, 2)
            act.dma_start(w1A_in[:, :], w1[0:DA, :]).then_inc(w1_here, 16)
            for i in range(2):
                act.dma_start(w1B_in[i * DB:(i + 1) * DB, :], w1[DA:D, :]).then_inc(w1_here, 16)

            def take_xn_hi(t, slot):
                complete(act, slot)
                ts, src = slice(t * TT, (t + 1) * TT), acc(slot[0])
                act.copy(xnA_hi[:, ts], src[:, 0:TT])
                for i in range(2):
                    cp = act.copy(xnB[i * DB:(i + 1) * DB, ts], src[0:DB, TT:2 * TT])
                cp.then_inc(xn_hi_ready, 1)

            def round_w1(b, part):
                cols = bass.ds(b * W1_PIECE, W1_PIECE)
                if part == 0:
                    act.wait_ge(w1_split, b + 1)
                    act.copy(w1B_part[:, :], w1B_in[0:DB, cols])
                elif part == 1:
                    act.copy(w1B[DB:2 * DB, cols], w1B_in[DB:2 * DB, cols])
                else:
                    act.copy(w1A_hi[:, cols], w1A_in[:, cols]).then_inc(w1_hi_ready, 1)

            def take_q(c, slot):
                complete(act, slot)
                act.copy(qT[:, c, :], acc(slot[0])[:, 0:BT]).then_inc(free[slot[0]], 1)

            def take_k(c, slot):
                complete(act, slot)
                src = acc(slot[0])
                for i in range(2):
                    rows_ = slice(DH * i, DH * (i + 1))
                    cp = act.copy(kT[rows_, c, i, :], src[rows_, 0:BT])
                cp.then_inc(free[slot[0]], 1)

            def exponentials(u, b):
                q, g, t0, n = unit(u)
                act.wait_ge(top_ready, NU * b + u + 1)
                for i in range(HQ):
                    head = probs[0:n, u % 3, i * n:(i + 1) * n]
                    ex = act.activation(head, head, ACT.Exp, bias=top[0:n, u % 3, i:i + 1],
                                        scale=LOGIT_SCALE, accum_out=total[0:n, u % 3, i:i + 1])
                ex.then_inc(exp_ready, 1)

            def take(w, c, slot):
                (take_q if w == "q" else take_k)(c, slot)

            for t in range(NT):
                take_xn_hi(t, product(("xt", t), 0, opening=True))
            act.wait_ge(kt_zero, 1)
            for c in range(2):
                for w in "qk":
                    take(w, c, product((w, c), 0, opening=True))

            def body(b, last):
                for s in range(NU + LAG_AV):
                    for key in step_products(s, last):
                        if key[0] in "qk" and key[1] > 1:
                            take(*key, product(key, b))
                    if LAG_T <= s < NU + LAG_T:
                        u = s - LAG_T
                        q, g, t0, n = unit(u)
                        act.wait_ge(tr_full, NU * b + u + 1)
                        act.copy(probsT[0:n, u % 3, 0:HQ * n], psum[0:n, TR_BANK, 0:HQ * n]).then_inc(tr_free, 1)
                    if s >= LAG_AV:
                        u = s - LAG_AV
                        q, g, t0, n = unit(u)
                        act.wait_ge(av_full, NU * b + u + 1)
                        src = psum[:, AV_BANK, 0:HQ * n].rearrange("p (c i n) -> p c i n", c=2, i=2)
                        for i in range(2):
                            rows_ = slice(DH * i, DH * (i + 1))
                            cp = act.copy(oT[rows_, 2 * q:2 * q + 2, t0:t0 + n], src[rows_, :, i, :])
                        cp.then_inc(av_free, 1)
                    if 1 <= s < NU - 1:
                        exponentials(s + 1, b)
                    for key in step_products(s, last):
                        if key[0] == "xt":
                            take_xn_hi(key[1], product(key, b))
                if not last:
                    round_w1(b, 0)
                    take("q", 0, product(("q", 0), b))
                    round_w1(b, 1)
                    for w, c in (("k", 0), ("q", 1), ("k", 1)):
                        take(w, c, product((w, c), b))
                for t in range(NT):
                    slot = product(("gt", t), b)
                    complete(act, slot)
                    act.copy(xn2A[:, t * TT:(t + 1) * TT], acc(slot[0])[:, 0:TT])
                    act.copy(xn2B[0:DB, t * TT:(t + 1) * TT],
                             acc(slot[0])[0:DB, TT:2 * TT]).then_inc(free[slot[0]], 1)
                if not last:
                    for u in range(AHEAD):
                        exponentials(u, b + 1)
                    round_w1(b, 2)

            for u in range(AHEAD):
                exponentials(u, 0)
            act.wait_ge(w1_here, 48)
            with act.Fori(0, NB - 1) as b:
                body(b, False)
            body(NB - 1, True)

            def round_x(r, i):
                j = r * 4 + i
                act.wait_ge(fxt_full, j + 1)
                act.copy(fxA_hi[i % 2], psum[0:DA, 7, 0:SLOT])
                for k in range(2):
                    cp = act.copy(fxB[i % 2][k * DB:(k + 1) * DB, :], psum[0:DB, 7, SLOT:2 * SLOT])
                cp.then_inc(fx_hi_ready, 1)

            act.activation(veps[:, 1, 0:1], minus_half[:, :], ACT.Gelu)

            def gelu(r, i):
                j = r * 4 + i
                for k, (lo, hi) in enumerate(((0, 512), (512, FF))):
                    act.wait_ge(biased, 2 * j + k + 1)
                    ge = act.activation(hid[i % 2][:, lo:hi], hid[i % 2][:, lo:hi], ACT.Gelu)
                ge.then_inc(hid_ready, 1)

            def take_hidden_rest(r, i):
                j = r * 4 + i
                act.wait_ge(hidt_full, 2 * j + 2)
                act.copy(hidT[i % 2][:, 512:FF], psum[:, 5, 0:FF - 512]).then_inc(hidt_rest_ready, 1)

            round_x(0, 0)
            round_x(0, 1)
            gelu(0, 0)
            round_x(0, 2)
            gelu(0, 1)

            def four_tiles(r, last):
                for i in range(4):
                    take_hidden_rest(r, i)
                    if not last or i < 2:
                        gelu(r, i + 2)
                    if not last or i < 1:
                        round_x(r, i + 3)

            with act.Fori(0, FFT // 4 - 1) as r:
                four_tiles(r, False)
            four_tiles(FFT // 4 - 1, True)

        @block.vector
        def _(dve):
            steps = [0, 0]

            def own(ins):
                ins.then_inc(dve_step, 1)
                steps[0] += 1
                dve.wait_ge(dve_step, steps[1] + steps[0])

            def layernorm_stats(src, kind, t):
                own(dve.bn_stats(stats[:, kind, t, :], src))
                passed("dve", dve)
                dve.bn_aggr(mv[:, kind, t, :], stats[:, kind, t, :]).then_inc(ln_stats, 1)

            def layernorm(dst, src, kind, t, n_before):
                dve.wait_ge(ln_rstd, n_before + 1)
                return dve.tensor_scalar(dst, src, mv[:, kind, t, 0:1], rstd[:, kind, t:t + 1],
                                         ALU.subtract, ALU.mult)

            def take_tokens(t, slot):
                complete(dve, slot)
                dve.tensor_tensor(h[:, t, :], acc(slot[0])[0:TT, 0:D], bias[:, :], ALU.add).then_inc(free[slot[0]], 1)
                taken(dve, slot)
                layernorm_stats(h[:, t, :], 0, t)

            def take_xn_lo(t, slot, n_before):
                dve.wait_ge(xn_hi_ready, n_before + 1)
                ts, src = slice(t * TT, (t + 1) * TT), acc(slot[0])
                dve.tensor_tensor(xnA_lo[:, ts], src[:, 0:TT], xnA_hi[:, ts], ALU.subtract)
                dve.tensor_tensor(xnB_lo[:, ts], src[0:DB, TT:2 * TT], xnB[0:DB, ts],
                                  ALU.subtract).then_inc(free[slot[0]], 1)

            def split_wq(i):
                cols = WQ_PIECES[i]
                dve.wait_ge(wq_hi_ready, 2 * i + 1)
                dve.tensor_tensor(wqA_lo[:, cols], wqA_in[:, cols], wqA_hi[:, cols], ALU.subtract).then_inc(wq_split, 1)
                dve.wait_ge(wq_hi_ready, 2 * i + 2)
                dve.tensor_tensor(wqB[DB:2 * DB, cols], wqB_in[0:DB, cols], wqB[0:DB, cols],
                                  ALU.subtract).then_inc(wq_split, 1)

            def soften(u, b):
                q, g, t0, n = unit(u)
                dve.wait_ge(sc_full, NU * b + u + 1)
                sc = probs[0:n, u % 3, 0:HQ * n].rearrange("p (h n) -> p h n", n=n)
                dve.tensor_tensor(sc, psum[0:n, SC_BANK, 0:HQ * n].rearrange("p (h n) -> p h n", n=n),
                                  mask[0:n, 0:n].unsqueeze(1).to_broadcast([n, HQ, n]),
                                  ALU.add).then_inc(sc_free, 1)
                dve.wait_ge(sc_free, NU * b + u + 2)
                own(dve.tensor_reduce(top[0:n, u % 3, :], sc, AX.X, ALU.max))
                dve.tensor_scalar(top[0:n, u % 3, :], top[0:n, u % 3, :], -LOGIT_SCALE, None,
                                  ALU.mult).then_inc(top_ready, 1)

            def normalise(u, b):
                q, g, t0, n = unit(u)
                dve.wait_ge(exp_ready, NU * b + u + 1)
                own(dve.reciprocal(share[0:n, u % 3, :], total[0:n, u % 3, :]))
                ex = probs[0:n, u % 3, 0:HQ * n].rearrange("p (h n) -> p h n", n=n)
                dve.tensor_tensor(ex, ex, share[0:n, u % 3, :].unsqueeze(2).to_broadcast([n, HQ, n]),
                                  ALU.mult).then_inc(probs_ready, 1)

            def take_v(g, f, slot):
                t0, n = GROUPS[g]
                complete(dve, slot)
                dve.tensor_copy(v[0:n, g, f * (HD // 2):(f + 1) * (HD // 2)],
                                acc(slot[0])[0:n, 0:HD // 2]).then_inc(free[slot[0]], 1)

            dve.sem_inc(sc_free, 1)
            dve.sem_inc(rows_ready, 1)
            dve.sem_inc(hidt_ready, 1)
            dve.sem_inc(y_ready, 1)
            dve.memset(xn2B[DB:DB + 1, :], 1.0)
            dve.memset(kT[:, :, :, :], 0.0).then_inc(kt_zero, 1)
            dve.wait_ge(wp_here, 32)
            for r in range(REPR):
                for c in range(CHANNELS - 1):
                    s = r * CHANNELS + c
                    if r == 0:
                        ins = dve.tensor_scalar(weff[:, c, :, :], wp[:, :, r, :], wr[:, s:s + 1], None, ALU.mult)
                    else:
                        ins = dve.scalar_tensor_tensor(weff[:, c, :, :], wp[:, :, r, :], wr[:, s:s + 1],
                                                       weff[:, c, :, :], ALU.mult, ALU.add)
                own(ins)
            dve.engine_nop().then_inc(weff_ready, 1)
            dve.wait_ge(br_here, 32)
            for r in range(REPR):
                if r == 0:
                    ins = dve.tensor_scalar(wb[:, :, :], wp[:, :, r, :], br[:, r:r + 1], None, ALU.mult)
                else:
                    ins = dve.scalar_tensor_tensor(wb[:, :, :], wp[:, :, r, :], br[:, r:r + 1], wb[:, :, :],
                                                   ALU.mult, ALU.add)
                own(ins)
            dve.engine_nop().then_inc(wb_ready, 1)
            split_wq(0)
            slot = product(("bias",), 0, opening=True)
            complete(dve, slot)
            dve.tensor_copy(bias[:, :], acc(slot[0])[0:TT, 0:D]).then_inc(free[slot[0]], 1)
            taken(dve, slot)
            for t in range(NT):
                take_tokens(t, product(("tok", t), 0, opening=True))
            for t in range(NT):
                layernorm(xn[:, t, :], h[:, t, :], 0, t, t).then_inc(xn_ready, 1)
            for t in range(NT):
                take_xn_lo(t, product(("xt", t), 0, opening=True), t)
            split_wq(1)
            dve.wait_ge(consts_ready, 1)
            own(dve.tensor_copy(iota[:, :], iota_i[:, :]))
            dve.tensor_scalar(filled[:, :], iota[:, 0:EXPERTS], float(TOKENS), None, ALU.mult)
            own(dve.tensor_copy(tok_f[:, :], tok_i[:, :]))
            for g in range(3):
                for f in range(2):
                    take_v(g, f, product(("v", g, f), 0, opening=True))
                    if g == 0:
                        soften(f, 0)
            before_blocks = steps[0]

            def body(b, last):
                steps[0] = 0
                steps[1] = before_blocks + b * OWN_PER_BLOCK
                lns = NT + b * 2 * NT

                for s in range(NU):
                    if 1 <= s < NU - 1:
                        soften(s + 1, b)
                    normalise(s, b)
                    if not last:
                        if 5 <= s < 8:
                            t = s - 5
                            if t == 0:
                                dve.wait_ge(rows_sent, 16 * b + 16)
                            layernorm(xn[:, t, :], h[:, t, :], 0, t, lns + t).then_inc(xn_ready, 1)
                        if 4 <= s < 7:
                            if s == 4:
                                dve.wait_ge(hres_ready, b + 1)
                            take_tokens(s - 4, product(("tok", s - 4), b))
                if not last:
                    for t in range(NT):
                        take_xn_lo(t, product(("xt", t), b), NT * b + NT + t)
                if last:
                    lns -= NT
                if last:
                    dve.wait_ge(hres_ready, NB)
                    dve.wait_ge(rows_sent, 16 * b + 16)
                for t in range(NT + 1):
                    if t < NT:
                        slot = product(("o", t), b)
                        complete(dve, slot)
                        dve.tensor_tensor(rows[:, t, 0:D], acc(slot[0])[0:TT, 0:D], hres[:, t, :],
                                          ALU.add).then_inc(free[slot[0]], 1)
                        taken(dve, slot)
                        layernorm_stats(rows[:, t, 0:D], 1, t)
                    if t >= 1:
                        layernorm(rows[:, t - 1, D:2 * D], rows[:, t - 1, 0:D], 1, t - 1,
                                  lns + NT + t - 1).then_inc(rows_ready, 1)
                if not last:
                    for g, f in ((0, 0), (0, 1), (1, 0)):
                        take_v(g, f, product(("v", g, f), b))
                        if g == 0:
                            soften(f, b + 1)
                slot = product(("lg",), b)
                complete(dve, slot)
                dve.tensor_copy(lg[:, :, :].rearrange("p t e -> p (t e)"),
                                acc(slot[0])[0:TT, 0:NT * EXPERTS]).then_inc(free[slot[0]], 1)
                taken(dve, slot)
                passed("dve", dve)
                for t in range(NT):
                    ins = dve.max(lgmax[:, t, :], lg[:, t, :])
                own(ins)
                passed("dve", dve)
                for t in range(NT):
                    ins = dve.max_index(lgidx[:, t, :], lgmax[:, t, :], lg[:, t, :])
                own(ins)
                own(dve.tensor_copy(chosen[:, :], lgidx[:, :, 0]))
                dve.tensor_tensor(onehot[:, :, :], iota[:, 0:EXPERTS].unsqueeze(1).to_broadcast([TT, NT, EXPERTS]),
                                  chosen[:, :].unsqueeze(2).to_broadcast([TT, NT, EXPERTS]),
                                  ALU.is_equal).then_inc(onehot_ready, 1)
                if not last:
                    for g, f in ((1, 1), (2, 0), (2, 1)):
                        take_v(g, f, product(("v", g, f), b))
                slot = product(("rk",), b)
                complete(dve, slot)
                rk = acc(slot[0])
                own(dve.tensor_tensor(place[:, :, :], rk[0:TT, 0:NT * EXPERTS].rearrange("p (t e) -> p t e", t=NT),
                                      filled[:, :].unsqueeze(1).to_broadcast([TT, NT, EXPERTS]), ALU.add))
                dve.tensor_tensor(filled[:, :], rk[0:TT, NT * EXPERTS:(NT + 1) * EXPERTS], filled[:, :],
                                  ALU.add).then_inc(free[slot[0]], 1)
                own(dve.tensor_tensor(place[:, :, :], place[:, :, :], onehot[:, :, :], ALU.mult))
                own(dve.tensor_reduce(place_f[:, :], place[:, :, :], AX.X, ALU.add))
                dve.wait_ge(lists_sent, 16 * NT * (b + 1))
                dve.tensor_copy(tok_id[:, :], tok_f[:, :])
                dve.tensor_copy(place_i[:, :], place_f[:, :]).then_inc(place_ready, 1)
                own(dve.tensor_scalar(tok_f[:, :], tok_f[:, :], float(BT), None, ALU.add))
                if not last:
                    assert steps[0] == OWN_PER_BLOCK, steps[0]

            with dve.Fori(0, NB - 1) as b:
                body(b, False)
            body(NB - 1, True)

            e8 = iota[0:1, 0:EXPERTS]
            j16 = iota[0:1, 0:FFT].unsqueeze(2).to_broadcast([1, FFT, EXPERTS])

            def over_tiles(row):
                return row.unsqueeze(1).to_broadcast([1, FFT, EXPERTS])

            own(dve.scalar_tensor_tensor(cnt[:, :], e8, -float(TOKENS), filled[0:1, :], ALU.mult, ALU.add))
            own(dve.tensor_scalar(tr[:, 0:9], iota[0:1, 0:9], float(SLOT), None, ALU.mult))
            own(dve.tensor_tensor(steps9[:, :, :], cnt[:, :].unsqueeze(2).to_broadcast([1, EXPERTS, 9]),
                                  tr[:, 0:9].unsqueeze(1).to_broadcast([1, EXPERTS, 9]), ALU.is_gt))
            own(dve.tensor_reduce(ntile[:, :], steps9[:, :, :], AX.X, ALU.add))
            own(dve.tensor_tensor_scan(tend[:, :], ones[0:1, 0:EXPERTS], ntile[:, :], 0.0, ALU.mult, ALU.add))
            own(dve.tensor_tensor(off[:, :], tend[:, :], ntile[:, :], ALU.subtract))
            own(dve.tensor_scalar(off[:, :], off[:, :], -float(SLOT), None, ALU.mult))
            own(dve.scalar_tensor_tensor(off[:, :], e8, float(TOKENS), off[:, :], ALU.mult, ALU.add))
            own(dve.tensor_tensor(grid[:, :, :], over_tiles(tend[:, :]), j16, ALU.is_le))
            own(dve.tensor_reduce(te[:, :], grid[:, :, :], AX.X, ALU.add))
            own(dve.tensor_tensor(grid[:, :, :], over_tiles(e8), te[:, :].unsqueeze(2).to_broadcast([1, FFT, EXPERTS]),
                                  ALU.is_equal))
            own(dve.scalar_tensor_tensor(grid2[:, :, :], j16, float(SLOT), over_tiles(off[:, :]), ALU.mult, ALU.add))
            own(dve.tensor_tensor(grid2[:, :, :], grid2[:, :, :], grid[:, :, :], ALU.mult))
            own(dve.tensor_reduce(tr[:, :], grid2[:, :, :], AX.X, ALU.add))
            own(dve.tensor_scalar(tr2[:, :], te[:, :], float(EXPERTS), float(LISTS), ALU.is_ge, ALU.mult))
            own(dve.tensor_tensor(tr[:, :], tr[:, :], tr2[:, :], ALU.add))
            own(dve.tensor_scalar(te7[:, :], te[:, :], float(EXPERTS - 1), None, ALU.min))
            dve.tensor_copy(tile_row[:, :], tr[:, :])
            dve.memset(xnB_lo.bitcast(F32), 0.0)
            dve.tensor_copy(tile_expert[:, :], te7[:, :]).then_inc(tiles_ready, 1)
            dve.wait_ge(tiles_ready, 1)

            def take_x(r, i):
                j = r * 4 + i
                e = dve.value_load(tile_expert[0:1, bass.ds(j, 1)], min_val=0, max_val=EXPERTS - 1)
                dve.wait_ge(fx_hi_ready, j + 1)
                dve.tensor_tensor(fxA_lo[i % 2], psum[0:DA, 7, 0:SLOT], fxA_hi[i % 2], ALU.subtract)
                dve.tensor_tensor(fxB_lo[i % 2][DB:2 * DB, :], psum[0:DB, 7, SLOT:2 * SLOT], fxB[i % 2][0:DB, :],
                                  ALU.subtract).then_inc(fx_ready, 1)
                dve.tensor_tensor(res[i % 4], xg[i % 4][:, 0:D], b2s[:, bass.ds(e, 1), :].rearrange("p o d -> p (o d)"),
                                  ALU.add).then_inc(res_ready, 1)

            def add_b1(r, i):
                j = r * 4 + i
                e = dve.value_load(tile_expert[0:1, bass.ds(j, 1)], min_val=0, max_val=EXPERTS - 1)
                for k, (lo, hi) in enumerate(((0, 512), (512, FF))):
                    dve.wait_ge(up_full, 2 * j + k + 1)
                    dve.tensor_tensor(hid[i % 2][:, lo:hi], psum[:, 2 * (i % 2) + k, 0:hi - lo],
                                      b1s[:, bass.ds(e, 1), lo:hi].rearrange("p o f -> p (o f)"),
                                      ALU.add).then_inc(biased, 1)

            def take_hidden(r, i):
                j = r * 4 + i
                dve.wait_ge(hidt_full, 2 * j + 1)
                dve.tensor_copy(hidT[i % 2][:, 0:512], psum[:, 4, :]).then_inc(hidt_ready, 1)

            def finish(r, i):
                j = r * 4 + i
                dve.wait_ge(down_full, j + 1)
                dve.wait_ge(res_ready, j + 1)
                dve.wait_ge(yo_free, j + 1)
                dve.tensor_tensor(yo[i % 4], psum[:, 6, 0:D], res[i % 4], ALU.add).then_inc(y_ready, 1)

            dve.wait_ge(b2_here, 16)
            take_x(0, 0)
            take_x(0, 1)
            dve.wait_ge(b1_here, 32)
            add_b1(0, 0)
            take_x(0, 2)
            add_b1(0, 1)

            def four_tiles(r, last):
                for i in range(4):
                    take_hidden(r, i)
                    if not last or i < 2:
                        add_b1(r, i + 2)
                    if not last or i < 1:
                        take_x(r, i + 3)
                    finish(r, i)

            with dve.Fori(0, FFT // 4 - 1) as r:
                four_tiles(r, False)
            four_tiles(FFT // 4 - 1, True)

        @block.gpsimd
        def _(pool):
            pools = [0]

            def own(ins):
                ins.then_inc(pool_step, 1)
                pools[0] += 1
                pool.wait_ge(pool_step, pools[0])

            pool.sem_inc(yo_free, 4)
            pool.sem_inc(w1_split, 1)
            pool.memset(ones[:, :], 1.0)
            own(pool.memset(ident[:, :], 0.0))
            pool.affine_select(out=ident[:, :], in_=ident[:, :], compare_op=ALU.not_equal, fill=1.0, base=0,
                               pattern=[[-1, P]], channel_multiplier=1).then_inc(ident_ready, 1)
            pool.memset(mask[:, :], 0.0)
            pool.memset(before[:, :], 1.0)
            pool.memset(all1[:, :], 1.0)
            pool.memset(minus_half[:, :], -0.5)
            pool.memset(zeros[:, :], 0.0)
            pool.memset(spare[:, :], SPARE_ROW)
            pool.iota(iota_i[:, :], pattern=[[1, 16]], base=0, channel_multiplier=0)
            pool.iota(place_i[:, :], pattern=[[TT, NT]], base=LISTS, channel_multiplier=1)
            pool.memset(tok_id[:, :], SPARE_ROW).then_inc(place_ready, 1)
            own(pool.iota(tok_i[:, :], pattern=[[TT, NT]], base=0, channel_multiplier=1))
            for r in range(1, REPR):
                pool.wait_ge(scaled, r + 1)
                own(pool.tensor_tensor(weff[:, CHANNELS - 1, :, :], wp_last[:, 0, :, :] if r == 1 else
                                       weff[:, CHANNELS - 1, :, :], wp_last[:, r, :, :], ALU.add))
            pool.engine_nop().then_inc(weff_ready, 1)
            pool.affine_select(out=before[:, :], in_=before[:, :], compare_op=ALU.is_gt, fill=0.0, base=0,
                               pattern=[[1, TT]], channel_multiplier=-1)
            images = GMAX // PER_IMAGE
            m3 = mask[:, :].rearrange("p (j n) -> p j n", n=PER_IMAGE)
            own(pool.affine_select(out=m3, in_=m3, compare_op=ALU.is_ge, fill=MASKED, base=0,
                                   pattern=[[-PER_IMAGE, images], [0, PER_IMAGE]], channel_multiplier=1))
            pool.affine_select(out=m3, in_=m3, compare_op=ALU.is_ge, fill=MASKED, base=PER_IMAGE - 1,
                               pattern=[[PER_IMAGE, images], [0, PER_IMAGE]],
                               channel_multiplier=-1).then_inc(consts_ready, 1)

            def inverse_std(kind, t, n_before, n_own):
                pool.wait_ge(ln_stats, n_before + 1)
                passed("pool", pool)
                pool.tensor_scalar(veps[:, kind, t:t + 1], mv[:, kind, t, 1:2], EPS, None,
                                   ALU.add).then_inc(pool_step, 1)
                pool.wait_ge(pool_step, n_own)
                pool.tensor_tensor(rstd[:, kind, t:t + 1], veps[:, kind, t:t + 1], minus_half[:, :],
                                   ALU.pow).then_inc(ln_rstd, 1)

            consts = pools[0]
            for t in range(NT):
                inverse_std(0, t, t, consts + t + 1)

            def send_places(n):
                pool.wait_ge(place_ready, n + 1)
                passed("pool", pool)
                for t in range(NT):
                    pool.indirect_dma_start(out=perm,
                                            out_offset=bass.IndirectOffsetOnAxis(ap=place_i[:, t:t + 1], axis=0),
                                            in_=tok_id[:, t:t + 1], in_offset=None).then_inc(lists_sent, 16)

            pool.wait_ge(inits_out, 32)
            def body(b, last):
                lns = NT + b * 2 * NT
                send_places(b)
                if not last:
                    for t in range(NT):
                        inverse_std(0, t, lns + t, consts + lns + t + 1)
                after = lns + (0 if last else NT)
                for t in range(NT):
                    inverse_std(1, t, after + t, consts + after + t + 1)
                if not last:
                    keep_h(b + 1)
                    split_w1(b)

            def keep_h(b):
                pool.wait_ge(xn_ready, NT * b + NT)
                pool.wait_ge(rows_ready, NT * b + 1)
                passed("pool", pool)
                pool.tensor_copy(hres[:, :, :], h[:, :, :]).then_inc(hres_ready, 1)

            def split_w1(b):
                cols = bass.ds(b * W1_PIECE, W1_PIECE)
                pool.wait_ge(w1_hi_ready, b + 1)
                pool.tensor_tensor(w1A_lo[:, cols], w1A_in[:, cols], w1A_hi[:, cols],
                                   ALU.subtract).then_inc(w1A_split, 1)
                pool.wait_ge(w1A_split, b + 1)
                pool.tensor_tensor(w1B[0:DB, cols], w1B_in[0:DB, cols], w1B_part[:, :],
                                   ALU.subtract).then_inc(w1_split, 1)

            keep_h(0)
            with pool.Fori(0, NB - 1) as b:
                body(b, False)
            body(NB - 1, True)
            send_places(NB)

            def gather(j):
                pool.wait_ge(ids_here[j], 16)
                if j >= 4:
                    pool.wait_ge(res_ready, j - 3)
                pool.indirect_dma_start(out=xg[j % 4], out_offset=None, in_=table,
                                        in_offset=bass.IndirectOffsetOnAxis(ap=ids[:, j:j + 1], axis=0)
                                        ).then_inc(xg_here[j % 4], 16)

            for j in range(4):
                gather(j)
            for j in range(FFT):
                if j + 4 < FFT:
                    gather(j + 4)
                pool.wait_ge(y_ready, j + 2)
                pool.indirect_dma_start(out=out, out_offset=bass.IndirectOffsetOnAxis(ap=ids[:, j:j + 1], axis=0),
                                        in_=yo[j % 4], in_offset=None, bounds_check=TOKENS - 1,
                                        oob_is_err=False).then_inc(out_sent[j % 4], 16)
                if j >= 2:
                    pool.wait_ge(out_sent[(j - 2) % 4], 16 * ((j - 2) // 4 + 1))
                    pool.sem_inc(yo_free, 1)
            for j in (FFT - 2, FFT - 1):
                pool.wait_ge(out_sent[j % 4], 16 * (j // 4 + 1))


OWN_PER_BLOCK = 2 * NU + 2 * NT + 2 + 1 + 1 + 3


def kernel(x, L0_tok_W_repr, L0_tok_b_repr, L0_tok_W_proj, L0_tok_b_proj, L0_attn_W_qkv, L0_attn_W_out,
           L0_ffn_gate_w, L0_ffn_gate_b, L0_ffn_w1, L0_ffn_b1, L0_ffn_w2, L0_ffn_b2):
    from concourse import bacc
    from concourse.bass_utils import run_bass_kernel_spmd

    half = PATCH // 2
    per = IMAGES // NB
    arrays = {
        "xT": np.asarray(x).reshape(NB, per, CHANNELS, GRID, 2, half, GRID, PATCH)
        .transpose(0, 5, 7, 2, 4, 1, 3, 6).reshape(NB, P, KX, BT),
        "w_proj": np.asarray(L0_tok_W_proj).reshape(REPR, D, 2, P).transpose(3, 2, 0, 1),
        "w_repr": np.asarray(L0_tok_W_repr).reshape(REPR * CHANNELS),
        "b_repr": np.asarray(L0_tok_b_repr),
        "b_proj": np.asarray(L0_tok_b_proj),
        "w_qkv": np.asarray(L0_attn_W_qkv).T,
        "w_out": np.asarray(L0_attn_W_out).T.reshape(PAIRS, P, D).transpose(1, 0, 2),
        "gate_w": np.asarray(L0_ffn_gate_w),
        "gate_b": np.asarray(L0_ffn_gate_b).reshape(1, EXPERTS),
        "w1": np.asarray(L0_ffn_w1).transpose(1, 0, 2).reshape(D, EXPERTS * FF),
        "b1": np.asarray(L0_ffn_b1),
        "w2": np.asarray(L0_ffn_w2).reshape(EXPERTS, FCH, P, D).transpose(2, 0, 1, 3),
        "b2": np.asarray(L0_ffn_b2),
    }
    nc = bacc.Bacc("TRN2", target_bir_lowering=False, num_devices=1)
    args = []
    for name in arrays:
        arrays[name] = np.ascontiguousarray(arrays[name])
        args.append(nc.dram_tensor(name, arrays[name].shape, F32, kind="ExternalInput").ap())
    args.append(nc.dram_tensor("out", [TOKENS, D], F32, kind="ExternalOutput").ap())
    build(nc, *args)
    r = run_bass_kernel_spmd(nc, [arrays], core_ids=[0])
    return r.results[0]["out"].reshape(IMAGES, PER_IMAGE, D)
```
